# Optimizing a Trainium2 kernel written in Bass

```python
import numpy as np
import jax
import jax.numpy as jnp

def _softmax(x, axis=-1):
    return jax.nn.softmax(x, axis=axis)

def _gelu(x):
    return jax.nn.gelu(x, approximate=True)

def _silu(x):
    return jax.nn.silu(x)

def _sigmoid(x):
    return jax.nn.sigmoid(x)

def _layernorm(x, axis=-1, eps=1e-05):
    m = jnp.mean(x, axis=axis, keepdims=True)
    v = jnp.var(x, axis=axis, keepdims=True)
    return (x - m) / jnp.sqrt(v + eps)

def _scatter_add(tgt, idx, src, axis=0):
    return tgt.at[idx].add(src)

def _segment_sum(src, seg, n):
    return jax.ops.segment_sum(src, seg, n)
kernel_name = 'mk_gnn_preln_d2_gnn_r8_291909'

def setup_inputs(seed: int=0):
    np.random.seed(seed)
    _w = jnp.asarray

    def _rec_inputs():
        import jax
        import jax.numpy as jnp
        _gk = jax.random.key(seed)
        x = -0.0003713 + 1 * jax.random.normal(jax.random.fold_in(_gk, 1), (6250, 256), jnp.float32)
        _s = jax.random.randint(jax.random.fold_in(_gk, 2), (50000,), 0, 6250, jnp.int32)
        _d = jax.random.randint(jax.random.fold_in(_gk, 3), (50000,), 0, 6250, jnp.int32)
        _loop = jnp.arange(6250, dtype=jnp.int32)
        src = jnp.concatenate([_s, _d, _loop])
        dst = jnp.concatenate([_d, _s, _loop])
        _o = jnp.argsort(dst, stable=True)
        src = src[_o]
        dst = dst[_o]
        return (x, src, dst)
    x, src, dst = _rec_inputs()

    def _L0_gnn_setup():
        import jax, jax.numpy as jnp
        import numpy as np
        N_NODES = 6250
        N_EDGES = 100000
        D_IN = 256
        D_OUT = 64
        N_HEADS = 4
        key = jax.random.key(seed)
        k1, k2, k3, k4 = jax.random.split(key, 4)
        x = jax.random.normal(k1, (N_NODES, D_IN), dtype=jnp.float32)
        W = jax.random.normal(k2, (N_HEADS, D_IN, D_OUT), dtype=jnp.float32) * np.sqrt(2.0 / (D_IN + D_OUT))
        a = jax.random.normal(k3, (N_HEADS, 2 * D_OUT), dtype=jnp.float32) * np.sqrt(2.0 / (2 * D_OUT + 1))
        edge_index = jax.random.randint(k4, (N_EDGES, 2), 0, N_NODES, dtype=jnp.int32)
        return {'x': x, 'W': W, 'a': a, 'edge_index': edge_index}
    _L0_gnn_all = _L0_gnn_setup()
    _L0_gnn_in = {k: v for k, v in _L0_gnn_all.items() if k in ('W', 'a')}
    del _L0_gnn_all

    def _L1_gnn_setup():
        import jax, jax.numpy as jnp
        import numpy as np
        N_NODES = 6250
        N_EDGES = 100000
        D = 256
        GD_STEPS = 5
        key = jax.random.key(seed)
        k1, k2, k3, k4 = jax.random.split(key, 4)
        x = jax.random.normal(k1, (N_NODES, D), dtype=jnp.float32)
        edge_index = jax.random.randint(k2, (2, N_EDGES), 0, N_NODES, dtype=jnp.int64)
        scale = 1.0 / np.sqrt(D)
        W0 = jax.random.normal(k3, (GD_STEPS, D, D), dtype=jnp.float32) * scale
        W1 = jax.random.normal(k4, (GD_STEPS, D, D), dtype=jnp.float32) * scale
        return {'x': x, 'edge_index': edge_index, 'W0': W0, 'W1': W1}
    _L1_gnn_all = _L1_gnn_setup()
    _L1_gnn_in = {k: v for k, v in _L1_gnn_all.items() if k in ('W0', 'W1')}
    del _L1_gnn_all
    return {'x': x, 'src': src, 'dst': dst, 'L0_gnn_W': _L0_gnn_in['W'], 'L0_gnn_a': _L0_gnn_in['a'], 'L1_gnn_W0': _L1_gnn_in['W0'], 'L1_gnn_W1': _L1_gnn_in['W1']}

def reference(x, src, dst, L0_gnn_W, L0_gnn_a, L1_gnn_W0, L1_gnn_W1):
    import jax
    import jax.numpy as jnp

    def _L0_gnn_ref(x, W, a, edge_index):
        import jax, jax.numpy as jnp
        import numpy as np
        N_NODES = 6250
        N_EDGES = 100000
        D_IN = 256
        D_OUT = 64
        N_HEADS = 4
        rows = edge_index[:, 0]
        cols = edge_index[:, 1]
        h = jnp.einsum('nd,hdo->hno', x, W)
        a1, a2 = (a[:, :D_OUT], a[:, D_OUT:])
        s1 = jnp.einsum('hno,ho->hn', h, a1)
        s2 = jnp.einsum('hno,ho->hn', h, a2)
        e = jax.nn.leaky_relu(s1[:, rows] + s2[:, cols], negative_slope=0.2)
        seg_max = jax.vmap(lambda v: jax.ops.segment_max(v, rows, num_segments=N_NODES))(e)
        ex = jnp.exp(e - seg_max[:, rows])
        seg_sum = jax.vmap(lambda v: jax.ops.segment_sum(v, rows, num_segments=N_NODES))(ex)
        alpha = ex / seg_sum[:, rows]
        msg = alpha[:, :, None] * h[:, cols]
        out = jax.vmap(lambda m: jax.ops.segment_sum(m, rows, num_segments=N_NODES))(msg)
        out = jax.nn.relu(out)
        return jnp.transpose(out, (1, 0, 2)).reshape(N_NODES, N_HEADS * D_OUT)

    def _L1_gnn_ref(x, edge_index, W0, W1):
        import jax, jax.numpy as jnp
        import numpy as np
        N_NODES = 6250
        N_EDGES = 100000
        D = 256
        GD_STEPS = 5
        n = x.shape[0]
        row, col = (edge_index[0], edge_index[1])
        deg = jax.ops.segment_sum(jnp.ones((edge_index.shape[1],), dtype=x.dtype), col, num_segments=n)
        dinv = jnp.where(deg > 0, jax.lax.rsqrt(jnp.where(deg > 0, deg, 1.0)), 0.0)
        norm = (dinv[row] * dinv[col])[:, None]
        steps = W0.shape[0]
        for k in range(steps):
            agg = jax.ops.segment_sum(x[row] * norm, col, num_segments=n)
            x = x @ W0[k].T + agg @ W1[k].T
        return x
    edge_index = jnp.stack([src, dst])
    edge_index_t = jnp.stack([src, dst], axis=1)
    h = jnp.maximum(_layernorm(x, axis=-1), 0.0)
    x = x + _L0_gnn_ref(h, L0_gnn_W, L0_gnn_a, edge_index_t)
    h = jnp.maximum(_layernorm(x, axis=-1), 0.0)
    x = x + _L1_gnn_ref(h, edge_index, L1_gnn_W0, L1_gnn_W1)
    return x

_drawn_inputs = setup_inputs


def setup_inputs(seed=0):
    import zlib

    import numpy as np

    out = dict(_drawn_inputs(seed))
    spreads = {}
    factors = {}
    for name, (base, spread) in spreads.items():
        noise = np.random.default_rng([zlib.crc32(name.encode()), seed]).standard_normal(out[name].shape)
        drawn = base * np.exp(spread * noise) if base else spread * noise
        out[name] = jnp.asarray(drawn.astype(out[name].dtype))
    for name, factor in factors.items():
        out[name] = (out[name] * factor).astype(out[name].dtype)
    return out
```

```python
import concourse.bass as bass
from concourse import mybir

F32 = mybir.dt.float32
BF16 = mybir.dt.bfloat16
I32 = mybir.dt.int32
ALU = mybir.AluOpType
ACT = mybir.ActivationFunctionType
AX = mybir.AxisListType

P = 128
N, D = 6250, 256
HEADS, DH = 4, 64
E = 106250
LAYERS = 5
EPS = 1e-5
NT = -(-N // P)
LAST = N - (NT - 1) * P
ET = -(-E // P)
GROUP = 4
RING = 4
BODY = GROUP * RING
BODIES = -(-(ET + NT - 1) // BODY)
STEPS = BODIES * BODY
GROUPS = STEPS // GROUP
SC = -(-STEPS // P)
SPAD = SC * P
PER = 832
ROWS = PER
U = 7
NB = NT // U
HD = D + HEADS
PX = HD + HEADS
SU = 8
SGROUPS = PER // SU
FAR = 100000
NEG = -1e30
FULL, PART = (ET - 1) // P * P, (ET - 1) % P
REST = E - (ET - 1) * P
CREDIT = 4


def program(nc, x, src, dst, w_att, a_att, w0t, w1t, out):
    def sb(name, shape, dt=F32):
        return nc.alloc_sbuf_tensor(name, shape, dt)

    def dram(name, shape, dt=F32):
        return nc.dram_tensor(name, shape, dt, kind="Internal").ap()

    src_rows = dram("src_rows", (ROWS + 1, P), I32)
    dst_rows = dram("dst_rows", (ROWS + 1, P), I32)
    att_table = dram("att_table", (NT * P, HD))
    s2_table = dram("s2_table", (NT * P, HEADS))
    runmax_table = dram("runmax_table", (P * PER, HEADS))
    y_table = dram("y_table", (NT * P, D))

    X = sb("X", [P, NT, D])
    RES = sb("RES", [P, NT * D])
    ACC = sb("ACC", [P, NT + 1, HD])
    rows = sb("rows", [P, BODY, HD])
    onehot = sb("onehot", [P, 2, GROUP, P])
    onehotT = sb("onehotT", [P, GROUP, P])
    loc = sb("loc", [P, SPAD])
    gidx = sb("gidx", [P, SPAD], I32)
    gidx_now = sb("gidx_now", [P, RING, GROUP], I32)
    ntile = sb("ntile", [1, STEPS + GROUP], I32)
    wA = sb("wA", [P, 2, PX])
    wB = sb("wB", [P, 2, D])
    ybuf = sb("ybuf", [P, U, HD])
    tileS = sb("tileS", [P, 2, D])
    tileT = sb("tileT", [P, 2, 2, P])
    iota_free = sb("iota_free", [P, P])
    ident = sb("ident", [P, P])
    ones = sb("ones", [P, P])
    ones_b = sb("ones_b", [P, 1], BF16)
    zero = sb("zero", [P, 1])
    chunk_id = sb("chunk_id", [P, SC])
    small = sb("small", [P, 12, SC])
    small_i = sb("small_i", [P, 2, SC], I32)
    header = sb("header", [1, P], I32)
    degree = sb("degree", [P, NT + 1])
    dinv = sb("dinv", [P, NT])
    meanvar = sb("meanvar", [P, NT, 2])
    rstd = sb("rstd", [P, NT])
    shift = sb("shift", [P, NT])
    last_edge = sb("last_edge", [P, NT], I32)
    node_sc = sb("node_sc", [P, NT + 1, 2, HEADS])
    zs = sb("zs", [P, 4, GROUP, HEADS])
    carry = sb("carry", [P, 2, HEADS])
    carry_row = sb("carry_row", [HEADS, 3, P + 1])
    carry_in = sb("carry_in", [P, HEADS])

    accf = ACC[:].rearrange("p n f -> p (n f)")
    at = [0]

    def tmp(words):
        at[0] += words
        return accf[:, at[0] - words:at[0]]

    cmp = tmp(SC * SPAD // 2).bitcast(BF16).rearrange("p (c i) -> p c i", c=SC)
    srow = tmp(SPAD).bitcast(I32).rearrange("p (c e) -> p c e", c=SC)
    drow = tmp(SPAD).bitcast(I32).rearrange("p (c e) -> p c e", c=SC)
    srowf = tmp(SPAD).rearrange("p (c e) -> p c e", c=SC)
    drowf = tmp(SPAD).rearrange("p (c e) -> p c e", c=SC)
    iota_steps = tmp(SPAD)
    nrowf = tmp(SPAD)
    dchk = tmp(SPAD).bitcast(I32).rearrange("p (c e) -> p c e", c=SC)
    schk = tmp(SPAD).bitcast(I32).rearrange("p (c e) -> p c e", c=SC)
    a_bc = tmp(HEADS * 2 * DH)
    prod = tmp(D)
    s2e = RES[:, 0:PER * HEADS].rearrange("p (j h) -> p j h", h=HEADS)
    runmax = RES[:, PER * HEADS:2 * PER * HEADS].rearrange("p (j h) -> p j h", h=HEADS)
    o = 2 * PER * HEADS
    fresh = RES[:, o:o + PER]
    o += PER
    sidx = RES[:, o:o + PER + 2 * SU].bitcast(I32)
    o += PER + 2 * SU
    dcur = RES[:, o:o + PER].bitcast(I32)
    dprev = RES[:, o + PER:o + 2 * PER].bitcast(I32)
    o += 2 * PER

    def rest(words):
        nonlocal o
        o += words
        return RES[:, o - words:o]

    tri = rest(P)
    cum = rest(3 * NT).rearrange("p (k n) -> p k n", k=3)
    nbr_max = rest(NT * HEADS).rearrange("p (n h) -> p n h", h=HEADS)
    rden = rest(NT * HEADS).rearrange("p (n h) -> p n h", h=HEADS)
    s2_rows = rest(2 * SU * HEADS).rearrange("p (b u h) -> p b u h", b=2, u=SU)
    s2_idx = rest(2 * SU).bitcast(I32).rearrange("p (b u) -> p b u", b=2)
    stats = ybuf[:].rearrange("p u f -> p (u f)")[:, 0:NT * 6].rearrange("p (n k) -> p n k", k=6)
    res3 = RES[:].rearrange("p (n f) -> p n f", f=D)

    agg = nc.alloc_psum_tensor("agg", [P, GROUP, 512], F32)
    tps = nc.alloc_psum_tensor("tps", [P, 2, 512], F32)
    dps = nc.alloc_psum_tensor("dps", [P, 2, 512], F32)

    S = nc.alloc_semaphore
    cleared, consts = S("cleared"), S("consts")
    edge_in, x_in, w_in, a_in, rows_out, lay_in = S("edge_in"), S("x_in"), S("w_in"), S("a_in"), S("rows_out"), S("lay_in")
    dve_step, act_step, pool_step = S("dve_step"), S("act_step"), S("pool_step")
    cmp_ready, counts_ready, tidx_ready, steps_in, steps_f, stepsT = (
        S("cmp_ready"), S("counts_ready"), S("tidx_ready"), S("steps_in"), S("steps_f"), S("stepsT"))
    plan_ready = S("plan_ready")
    wext_ready = S("wext_ready")
    var_ready, std_ready, norm_ready = S("var_ready"), S("std_ready"), S("norm_ready")
    h_ready, h_tr, hT_ready, proj_ready, proj_copied, att_sent, batch_out, table1 = (
        S("h_ready"), S("h_tr"), S("hT_ready"), S("proj_ready"), S("proj_copied"), S("att_sent"), S("batch_out"), S("table1"))
    s2idx_ready, s2_saved = S("s2idx_ready"), S("s2_saved")
    s2_landed = [S("s2_landed0"), S("s2_landed1")]
    fresh_ready = S("fresh_ready")
    onehot_ready, step_summed, step_added = S("onehot_ready"), S("step_summed"), S("step_added")
    idx_ready = S("idx_ready")
    rows_landed = [S(f"rows_landed{h}") for h in range(RING)]
    deg_ready, cum_ready, pos_ready = S("deg_ready"), S("cum_ready"), S("pos_ready")
    carry_ready, carryT, carry_done, carry_back = S("carry_ready"), S("carryT"), S("carry_done"), S("carry_back")
    runmax_ready, runmax_out, nbr_in, sc_ready = S("runmax_ready"), S("runmax_out"), S("nbr_in"), S("sc_ready")
    ohT_ps, ohT_ready, edge_sc, z_ready, p_ready, weighted = (
        S("ohT_ps"), S("ohT_ready"), S("edge_sc"), S("z_ready"), S("p_ready"), S("weighted"))
    gap_ready = S("gap_ready")
    acc_free, acc_clear, res_ready = S("acc_free"), S("acc_clear"), S("res_ready")
    x0_ready, y_ready, y_sent, y_batch = S("x0_ready"), S("y_ready"), S("y_sent"), S("y_batch")
    table_ready = S("table_ready")
    w_layer = S("w_layer")
    z_copy, z_tr, z_copyT, z_ps, z_done = S("z_copy"), S("z_tr"), S("z_copyT"), S("z_ps"), S("z_done")
    passes_added = S("passes_added")
    g_copy, g_tr, g_copyT, g_ps, g_x = S("g_copy"), S("g_tr"), S("g_copyT"), S("g_ps"), S("g_x")
    out_ready, out_sent = S("out_ready"), S("out_sent")

    Q_DEG, Q_ATT, Q_LAYER = 0, 1, 2

    def step_tiles(engine, group):
        _, tiles = nc.values_load_multi_w_load_instructions(ntile[0:1, bass.ds(group * GROUP, GROUP)], engines=(engine,),
                                                            min_val=0, max_val=NT)
        return tiles

    with nc.Block() as block:

        @block.sync
        def _(sp):
            sp.nop(nofuse=True).then_inc(batch_out, 1)
            sp.nop(nofuse=True).then_inc(y_batch, 1)
            sp.wait_ge(cleared, 1)
            for v, chk in ((dst, dchk), (src, schk)):
                sp.dma_start(chk[:, 0:SC - 1, :], v[0:FULL * P].rearrange("(c p e) -> p c e", p=P, e=P)).then_inc(edge_in, 16)
                sp.dma_start(chk[0:PART, SC - 1, :], v[FULL * P:(FULL + PART) * P].rearrange("(p e) -> p e", e=P)).then_inc(edge_in, 16)
                sp.dma_start(chk[PART:PART + 1, SC - 1, 0:REST], v[(ET - 1) * P:E].rearrange("(p e) -> p e", p=1)).then_inc(edge_in, 16)
            sp.wait_ge(edge_in, 96)
            for r, chk in ((dst_rows, dchk), (src_rows, schk)):
                sp.dma_start(r[1:1 + FULL, :].rearrange("(c p) e -> p c e", p=P), chk[:, 0:SC - 1, :]).then_inc(rows_out, 16)
                sp.dma_start(r[1 + FULL:1 + ROWS, :], chk[0:ROWS - FULL, SC - 1, :]).then_inc(rows_out, 16)
                sp.dma_start(r[0:1, :], header[:]).then_inc(rows_out, 16)
            sp.dma_start(X[:, 0:NT - 1, :], x[0:(NT - 1) * P, :].rearrange("(n p) f -> p n f", p=P)).then_inc(x_in, 16)
            sp.dma_start(X[0:LAST, NT - 1, :], x[(NT - 1) * P:N, :]).then_inc(x_in, 16)
            sp.dma_start(wA[:, :, 0:D], w_att.rearrange("(c p) f -> p c f", p=P)).then_inc(w_in, 16)
            sp.dma_start(a_bc, a_att.rearrange("h o -> (h o)").partition_broadcast(P)).then_inc(a_in, 16)
            sp.wait_ge(rows_out, 96)
            sflat = src_rows.rearrange("r e -> (r e)")
            dflat = dst_rows.rearrange("r e -> (r e)")
            sp.dma_start(sidx[:, 0:PER], sflat[P:P + P * PER].rearrange("(p j) -> p j", p=P)).then_inc(lay_in, 16)
            sp.dma_start(dcur, dflat[P:P + P * PER].rearrange("(p j) -> p j", p=P)).then_inc(lay_in, 16)
            sp.dma_start(dprev, dflat[P - 1:P - 1 + P * PER].rearrange("(p j) -> p j", p=P)).then_inc(lay_in, 16)
            with sp.Fori(0, NB) as i:
                for u in range(U):
                    sp.wait_ge(proj_copied, i * U + u + 1 + 2)
                    sp.dma_start(att_table[bass.ds((i * U + u) * P, P), :], ybuf[:, u, :]).then_inc(att_sent, 16)
                    sp.dma_start(s2_table[bass.ds((i * U + u) * P, P), :], ybuf[:, u, D:HD]).then_inc(att_sent, 16)
                sp.wait_ge(att_sent, (i + 1) * (U * 32))
                sp.nop(nofuse=True).then_inc(batch_out, 1)
            sp.wait_ge(runmax_ready, 1)
            sp.dma_start(runmax_table.rearrange("(p j) h -> p j h", p=P), runmax).then_inc(runmax_out, 16)
            sp.dma_start(wB[:], w1t[0:1].rearrange("l (c p) f -> p (l c) f", p=P)).then_inc(w_layer, 16)
            sp.wait_ge(proj_ready, NT + 2)
            sp.dma_start(wA[:, :, 0:D], w0t[0:1].rearrange("l (c p) f -> p (l c) f", p=P)).then_inc(w_layer, 16)

            def send_y(k):
                with sp.Fori(0, NB) as i:
                    for u in range(U):
                        sp.wait_ge(y_ready, k * NT + i * U + u + 1)
                        sp.dma_start(y_table[bass.ds((i * U + u) * P, P), :], ybuf[:, u, 0:D]).then_inc(y_sent, 16)
                    sp.wait_ge(y_sent, (k * NB + i + 1) * (U * 16))
                    sp.nop(nofuse=True).then_inc(y_batch, 1)

            send_y(0)
            with sp.Fori(1, LAYERS) as k:
                send_y(k)
                sp.wait_ge(g_ps, k * NT + 2)
                sp.dma_start(wA[:, :, 0:D], w0t[bass.ds(k, 1)].rearrange("l (c p) f -> p (l c) f", p=P)).then_inc(w_layer, 16)
                sp.dma_start(wB[:], w1t[bass.ds(k, 1)].rearrange("l (c p) f -> p (l c) f", p=P)).then_inc(w_layer, 16)
            send_y(LAYERS)
            for c in range(U):
                sp.wait_ge(out_ready, c + 1)
                t0, t1 = c * NB, (c + 1) * NB
                if c < U - 1:
                    sp.dma_start(out[t0 * P:t1 * P, :].rearrange("(n p) f -> p n f", p=P), X[:, t0:t1, :]).then_inc(out_sent, 16)
                else:
                    sp.dma_start(out[t0 * P:(NT - 1) * P, :].rearrange("(n p) f -> p n f", p=P), X[:, t0:NT - 1, :]).then_inc(out_sent, 16)
                    sp.dma_start(out[(NT - 1) * P:N, :], X[0:LAST, NT - 1, :]).then_inc(out_sent, 16)
            sp.wait_ge(out_sent, 16 * (U + 1))

        @block.gpsimd
        def _(pool):
            pool.iota(iota_free[:], [[1, P]], base=0, channel_multiplier=0, allow_small_or_imprecise_dtypes=True)
            pool.iota(iota_steps, [[1, SPAD]], base=0, channel_multiplier=0, allow_small_or_imprecise_dtypes=True)
            pool.iota(chunk_id[:], [[P, SC]], base=0, channel_multiplier=1, allow_small_or_imprecise_dtypes=True)
            pool.memset(ident[:], 0.0)
            pool.memset(tri, 1.0).then_inc(pool_step, 1)
            pool.wait_ge(pool_step, 1)
            pool.affine_select(out=ident[:], in_=ident[:], compare_op=ALU.not_equal, fill=1.0, base=0,
                               pattern=[[-1, P]], channel_multiplier=1)
            pool.affine_select(out=tri, in_=tri, compare_op=ALU.is_ge, fill=0.0, base=0,
                               pattern=[[1, P]], channel_multiplier=-1).then_inc(consts, 1)
            pool.wait_ge(rows_out, 96)
            pool.wait_ge(tidx_ready, 1)
            for c in range(SC):
                at_c = bass.IndirectOffsetOnAxis(ap=small_i[:, 1, c:c + 1], axis=0)
                pool.indirect_dma_start(srow[:, c, :], None, src_rows, at_c).then_inc(steps_in, 16)
                pool.indirect_dma_start(drow[:, c, :], None, dst_rows, at_c).then_inc(steps_in, 16)
            pool.wait_ge(batch_out, NB + 1)
            with pool.Fori(0, SGROUPS // 2) as i:
                for h in range(2):
                    pool.wait_ge(s2idx_ready, 2 * i + h + 1)
                    pool.nop(nofuse=True)
                    for u in range(SU):
                        pool.indirect_dma_start(s2_rows[:, h, u, :], None, s2_table,
                                                bass.IndirectOffsetOnAxis(ap=s2_idx[:, h, u:u + 1], axis=0)).then_inc(s2_landed[h], 16)
            pool.wait_ge(runmax_out, 16)
            pool.wait_ge(pos_ready, 1)
            for n in range(NT):
                pool.indirect_dma_start(nbr_max[:, n, :], None, runmax_table,
                                        bass.IndirectOffsetOnAxis(ap=last_edge[:, n:n + 1], axis=0)).then_inc(nbr_in, 16)

            def gather(q, table, width):
                with pool.Fori(0, BODIES) as i:
                    for h in range(RING):
                        pool.wait_ge(idx_ready, (q * BODIES + i) * RING + h + 1)
                        pool.nop(nofuse=True)
                        for u in range(GROUP):
                            pool.indirect_dma_start(rows[:, h * GROUP + u, 0:width], None, table,
                                                    bass.IndirectOffsetOnAxis(ap=gidx_now[:, h, u:u + 1], axis=0)).then_inc(rows_landed[h], 16)

            gather(0, att_table, HD)
            pool.wait_ge(acc_free, 1)
            pool.memset(ACC[:], 0.0).then_inc(acc_clear, 1)
            with pool.Fori(1, LAYERS + 1) as k:
                pool.wait_ge(y_batch, k * NB + 1)
                pool.nop(nofuse=True)
                gather(k, y_table, D)
                with pool.Fori(0, NT) as n:
                    pool.wait_ge(g_copy, (k - 1) * NT + n + 1)
                    pool.nop(nofuse=True)
                    pool.tensor_copy(ACC[:, bass.ds(n, 1), 0:D], zero[:, 0:1].unsqueeze(2).broadcast_to([P, 1, D])).then_inc(acc_clear, 1)

        @block.scalar
        def _(act):
            act.nop(nofuse=True).then_inc(hT_ready, 2)
            act.nop(nofuse=True).then_inc(g_copyT, 2)
            act.wait_ge(var_ready, 1)
            act.activation(rstd[:], rstd[:], ACT.Sqrt).then_inc(std_ready, 1)
            act.wait_ge(norm_ready, 1)
            with act.Fori(0, NB) as i:
                def normalise(u):
                    n = i * U + u
                    act.wait_ge(h_tr, n + (2 if u == 0 else 1))
                    act.nop(nofuse=True)
                    act.activation(tileS[:, u % 2, :], X[:, bass.ds(n, 1), :], ACT.Relu, bias=shift[:, bass.ds(n, 1)],
                                   scale=rstd[:, bass.ds(n, 1)]).then_inc(h_ready, 1)

                normalise(0)
                for u in range(U):
                    n = i * U + u
                    if u + 1 < U:
                        normalise(u + 1)
                    act.wait_ge(h_tr, n + 3)
                    act.wait_ge(proj_ready, n + (2 if u == 0 else 1))
                    act.activation(tileT[:, u % 2, :, :], tps[:, u % 2, 0:D].rearrange("p (c m) -> p c m", c=2), ACT.Copy).then_inc(hT_ready, 1)
            act.wait_ge(lay_in, 48)
            for h in range(2):
                act.activation(s2_idx[:, h, :], sidx[:, h * SU:(h + 1) * SU], ACT.Copy).then_inc(s2idx_ready, 1)
            with act.Fori(0, SGROUPS // 2) as i:
                for h in range(2):
                    act.wait_ge(s2_landed[h], (i + 1) * (16 * SU))
                    act.nop(nofuse=True)
                    act.activation(s2e[:, bass.ds((2 * i + h) * SU, SU), :], s2_rows[:, h, :, :], ACT.Copy).then_inc(s2_saved, 1)
                    act.activation(s2_idx[:, h, :], sidx[:, bass.ds((2 * i + h + 2) * SU, SU)], ACT.Copy).then_inc(s2idx_ready, 1)
            act.wait_ge(plan_ready, 1)
            act.activation(dinv[:], cum[:, 2, :], ACT.Sqrt).then_inc(std_ready, 1)
            for h in range(RING):
                act.activation(gidx_now[:, h, :], gidx[:, h * GROUP:(h + 1) * GROUP], ACT.Copy).then_inc(idx_ready, 1)

            def next_index(q, i, h):
                act.wait_ge(step_summed, ((q * BODIES + i) * RING + h + 1) * GROUP + CREDIT)
                act.nop(nofuse=True)
                act.activation(gidx_now[:, h, :], gidx[:, bass.ds((i * RING + h + RING) * GROUP, GROUP)], ACT.Copy).then_inc(idx_ready, 1)

            def ohT_copy(j):
                act.wait_ge(ohT_ps, j + 1)
                act.activation(onehotT[:].rearrange("p g m -> p (g m)"), tps[:, 0, :], ACT.Copy).then_inc(ohT_ready, 1)

            ohT_copy(0)
            with act.Fori(0, BODIES) as i:
                for h in range(RING):
                    j = i * RING + h
                    act.wait_ge(z_ready, j + 1)
                    act.activation(zs[:, 3, :, :], zs[:, 2, :, :], ACT.Relu).then_inc(gap_ready, 1)
                    act.wait_ge(gap_ready, j + 1)
                    act.activation(rows[:, h * GROUP:(h + 1) * GROUP, D:HD], zs[:, 3, :, :], ACT.Exp, scale=-1.0).then_inc(p_ready, 1)
                    ohT_copy(j + 1)
                    next_index(Q_ATT, i, h)
            act.wait_ge(var_ready, 2)
            act.activation(rstd[:], rstd[:], ACT.Sqrt).then_inc(std_ready, 1)
            act.wait_ge(norm_ready, 2)
            with act.Fori(0, NT) as n:
                act.activation(X[:, bass.ds(n, 1), :], res3[:, bass.ds(n, 1), :], ACT.Relu, bias=shift[:, bass.ds(n, 1)],
                               scale=rstd[:, bass.ds(n, 1)]).then_inc(x0_ready, 1)
            act.wait_ge(x0_ready, NT)
            with act.Fori(1, LAYERS + 1) as k:
                act.wait_ge(g_x, (k - 1) * NT + 2)
                act.nop(nofuse=True)

                def body(i, dense):
                    for h in range(RING):
                        next_index(Q_LAYER - 1 + k, i, h)
                        m = k * NT - NT + i
                        if dense and h == 0:
                            act.activation(tileS[:, 0, :], X[:, bass.ds(i, 1), :], ACT.Copy).then_inc(z_copy, 1)
                        if dense and h == 1:
                            act.wait_ge(z_tr, m + 1)
                            act.activation(tileT[:, 0, :, :], tps[:, 0, 0:D].rearrange("p (c m) -> p c m", c=2), ACT.Copy).then_inc(z_copyT, 1)
                        if dense and h == 2:
                            act.wait_ge(z_ps, m + 1)
                            act.nop(nofuse=True)
                            act.activation(X[:, bass.ds(i, 1), :], dps[:, 0, 0:D], ACT.Copy).then_inc(z_done, 1)

                with act.Fori(0, NT) as i:
                    body(i, True)
                with act.Fori(NT, BODIES) as i:
                    body(i, False)
                act.wait_ge(passes_added, k)
                act.nop(nofuse=True)
                with act.Fori(0, NB) as i:
                    def scale_sums(u):
                        n = i * U + u
                        act.wait_ge(g_tr, (k - 1) * NT + n + (2 if u == 0 else 1))
                        act.nop(nofuse=True)
                        act.activation(tileS[:, u % 2, :], ACC[:, bass.ds(n, 1), 0:D], ACT.Copy, scale=dinv[:, bass.ds(n, 1)]).then_inc(g_copy, 1)

                    scale_sums(0)
                    for u in range(U):
                        m = (k - 1) * NT + i * U + u
                        if u + 1 < U:
                            scale_sums(u + 1)
                        act.wait_ge(g_tr, m + 3)
                        act.wait_ge(g_ps, m + (2 if u == 0 else 1))
                        act.activation(tileT[:, u % 2, :, :], tps[:, u % 2, 0:D].rearrange("p (c m) -> p c m", c=2), ACT.Copy).then_inc(g_copyT, 1)

        @block.vector
        def _(dve):
            links = [0]

            def link(ins):
                links[0] += 1
                ins.then_inc(dve_step, 1)
                dve.wait_ge(dve_step, links[0])

            nc.vector.memset(dchk[:, SC - 1, :], FAR)
            nc.vector.memset(schk[:, SC - 1, :], 0)
            nc.vector.memset(header[:], -1)
            nc.vector.memset(X[:, NT - 1, :], 0.0)
            nc.vector.memset(sidx[:, PER:PER + 2 * SU], 0)
            nc.vector.memset(ones[:], 1.0)
            nc.vector.memset(ones_b[:], 1.0)
            nc.vector.memset(zero[:], 0.0)
            nc.vector.memset(node_sc[:], 0.0)
            nc.vector.memset(degree[:], 0.0).then_inc(cleared, 1)
            dve.engine_nop().then_inc(proj_copied, 2)

            def layernorm(tiles):
                with dve.Fori(0, NT) as n:
                    nc.vector.bn_stats(stats[:, bass.ds(n, 1), :], tiles[:, bass.ds(n, 1), :])
                link(dve.engine_nop())
                mean, var = meanvar[:, :, 0], meanvar[:, :, 1]
                link(nc.vector.tensor_tensor(var, stats[:, :, 1], stats[:, :, 4], ALU.subtract))
                link(nc.vector.tensor_tensor(var, var, var, ALU.mult))
                link(nc.vector.tensor_scalar(var, var, 0.25, EPS, ALU.mult, ALU.add))
                link(nc.vector.tensor_tensor(mean, stats[:, :, 2], stats[:, :, 5], ALU.add))
                link(nc.vector.scalar_tensor_tensor(rstd[:], mean, 1.0 / D, var, ALU.mult, ALU.add))
                link(nc.vector.tensor_tensor(mean, stats[:, :, 1], stats[:, :, 4], ALU.add))
                nc.vector.tensor_scalar(mean, mean, 0.5, None, ALU.mult).then_inc(var_ready, 1)

            def layernorm_end(count):
                dve.wait_ge(std_ready, count)
                link(nc.vector.reciprocal(rstd[:], rstd[:]))
                link(nc.vector.tensor_tensor(shift[:], meanvar[:, :, 0], rstd[:], ALU.mult))
                nc.vector.tensor_scalar(shift[:], shift[:], -1.0, None, ALU.mult).then_inc(norm_ready, 1)

            dve.wait_ge(edge_in, 96)
            dve.wait_ge(consts, 1)
            link(nc.vector.tensor_single_scalar(small_i[:, 0, :], dchk[:, :, 0], 7, ALU.arith_shift_right))
            link(nc.vector.tensor_copy(small[:, 0, :], small_i[:, 0, :]))
            link(nc.vector.tensor_tensor(small[:, 1, :], small[:, 0, :], chunk_id[:], ALU.add))
            link(nc.vector.tensor_scalar(small[:, 2, :], chunk_id[:], 0.0, None, ALU.is_gt))
            link(nc.vector.tensor_tensor(small[:, 3, :], small[:, 1, :], small[:, 2, :], ALU.mult))
            for c in range(SC):
                last = nc.vector.tensor_scalar(cmp[:, c, :], iota_steps, small[:, 3, c:c + 1], None, ALU.is_ge)
            last.then_inc(cmp_ready, 1)
            dve.wait_ge(counts_ready, 1)
            link(nc.vector.tensor_copy(small[:, 4, :], dps[:, 0, 0:SC]))
            nc.vector.tensor_copy(small_i[:, 1, :], small[:, 4, :]).then_inc(tidx_ready, 1)
            link(nc.vector.tensor_tensor(small[:, 5, :], chunk_id[:], small[:, 4, :], ALU.subtract))
            link(nc.vector.tensor_scalar(small[:, 6, :], small[:, 5, :], 1.0, -float(P), ALU.add, ALU.mult))
            HS = SPAD // 2
            for b in range(2):
                last = nc.vector.tensor_tensor(nrowf[0:1, b * HS:(b + 1) * HS], iota_steps[0:1, b * HS:(b + 1) * HS],
                                               tps[0:1, b, 0:HS], ALU.subtract)
            link(last)
            nc.vector.tensor_scalar(ntile[:, 0:STEPS], nrowf[0:1, 0:STEPS], 1.0, None, ALU.add)
            link(nc.vector.tensor_scalar(ntile[:, STEPS:STEPS + GROUP], nrowf[0:1, 0:GROUP], 1.0, None, ALU.add))
            dve.wait_ge(w_in, 16)
            dve.wait_ge(a_in, 16)
            a4 = a_bc.rearrange("p (h s o) -> p h s o", h=HEADS, s=2)
            pr = prod.rearrange("p (h o) -> p h o", h=HEADS)
            for c in range(2):
                for half, col in ((1, D), (0, HD)):
                    link(nc.vector.tensor_tensor(pr, wA[:, c, 0:D].rearrange("p (h o) -> p h o", h=HEADS), a4[:, :, half, :], ALU.mult))
                    link(nc.vector.tensor_reduce(wA[:, c, col:col + HEADS], pr, AX.X, ALU.add))
            dve.engine_nop().then_inc(wext_ready, 1)
            dve.wait_ge(x_in, 32)
            layernorm(X)
            layernorm_end(1)
            dve.wait_ge(steps_in, 16 * 2 * SC)
            nc.vector.tensor_copy(srowf, srow)
            link(nc.vector.tensor_copy(drowf, drow))
            for c in range(SC):
                last = nc.vector.tensor_scalar(drowf[:, c, :], drowf[:, c, :], small[:, 6, c:c + 1], None, ALU.add)
            last.then_inc(steps_f, 1)
            dve.wait_ge(stepsT, 1)
            for b in range(2):
                w = (min(SC, 4 * b + 4) - 4 * b) * P
                nc.vector.tensor_copy(loc[:, b * 512:b * 512 + w], agg[:, b, 0:w])
                last = nc.vector.tensor_copy(gidx[:, b * 512:b * 512 + w], agg[:, 2 + b, 0:w])
            link(last)
            nc.vector.tensor_copy(loc[:, STEPS:SPAD], loc[:, 0:SPAD - STEPS])
            link(nc.vector.tensor_copy(gidx[:, STEPS:SPAD], gidx[:, 0:SPAD - STEPS]))
            dve.wait_ge(lay_in, 48)
            link(nc.vector.tensor_tensor(fresh, dcur, dprev, ALU.not_equal))
            link(nc.vector.tensor_scalar(fresh, fresh, NEG, None, ALU.mult))
            with dve.Fori(0, NB) as i:
                dve.wait_ge(batch_out, i + 1)
                dve.nop(nofuse=True)
                for u in range(U):
                    n = i * U + u
                    dve.wait_ge(proj_ready, n + 3)
                    nc.vector.tensor_copy(ybuf[:, u, :], dps[:, u % 2, 0:HD])
                    nc.vector.tensor_copy(node_sc[:, bass.ds(n, 1), 0, :], dps[:, u % 2, HD:PX]).then_inc(proj_copied, 1)

            def make_onehot(J, col, slot):
                dve.wait_ge(step_summed, (J - 1) * GROUP + CREDIT)
                nc.vector.tensor_tensor(onehot[:, slot, :, :], iota_free[:].unsqueeze(1).broadcast_to([P, GROUP, P]),
                                        loc[:, bass.ds(col, GROUP)].unsqueeze(2).broadcast_to([P, GROUP, P]),
                                        ALU.is_equal).then_inc(onehot_ready, 1)

            def add_steps(q, i, h, target, width):
                tiles = step_tiles(mybir.EngineType.DVE, i * RING + h)
                for s, n in enumerate(tiles):
                    g = ((q * BODIES + i) * RING + h) * GROUP + s
                    dve.wait_ge(step_summed, g + 1 + CREDIT)
                    dve.wait_ge(step_added, g + CREDIT)
                    nc.vector.tensor_tensor(target(n), target(n), agg[:, s, 0:width], ALU.add).then_inc(step_added, 1)

            dve.engine_nop().then_inc(step_added, CREDIT)
            nc.vector.tensor_tensor(onehot[:, 0, :, :], iota_free[:].unsqueeze(1).broadcast_to([P, GROUP, P]),
                                    loc[:, 0:GROUP].unsqueeze(2).broadcast_to([P, GROUP, P]), ALU.is_equal).then_inc(onehot_ready, 1)
            with dve.Fori(0, BODIES) as i:
                for h in range(RING):
                    make_onehot((Q_DEG * BODIES + i) * RING + h + 1, (i * RING + h + 1) * GROUP, (h + 1) % 2)
                    add_steps(Q_DEG, i, h, lambda n: degree[:, bass.ds(n, 1)], 1)
            dve.engine_nop().then_inc(deg_ready, 1)
            dve.wait_ge(cum_ready, 1)
            link(nc.vector.tensor_copy(cum[:, 0, :], dps[:, 1, 0:NT]))
            link(nc.vector.tensor_tensor_scan(cum[:, 1, :], ones[:, 0:NT], cum[:, 0, :], 0.0, ALU.mult, ALU.add))
            link(nc.vector.tensor_tensor(cum[:, 1, :], cum[:, 1, :], cum[:, 0, :], ALU.subtract))
            link(nc.vector.tensor_tensor(cum[:, 1, :], cum[:, 1, :], dps[:, 0, 0:NT], ALU.add))
            nc.vector.tensor_scalar(last_edge[:], cum[:, 1, :], -1.0, 0.0, ALU.add, ALU.max).then_inc(pos_ready, 1)
            nc.vector.tensor_scalar(cum[:, 2, :], degree[:, 0:NT], 1.0, None, ALU.max).then_inc(plan_ready, 1)
            dve.wait_ge(std_ready, 2)
            link(nc.vector.reciprocal(dinv[:], dinv[:]))
            link(nc.vector.tensor_scalar(cum[:, 0, :], degree[:, 0:NT], 0.0, None, ALU.is_gt))
            link(nc.vector.tensor_tensor(dinv[:], dinv[:], cum[:, 0, :], ALU.mult))
            dve.wait_ge(s2_saved, SGROUPS)
            for hd in range(HEADS):
                last = nc.vector.tensor_tensor_scan(runmax[:, :, hd], fresh, s2e[:, :, hd], NEG, ALU.add, ALU.max)
            link(last)
            nc.vector.tensor_copy(carry[:, 0, :], runmax[:, PER - 1, :])
            link(nc.vector.tensor_reduce(carry_in[:, 0:1], fresh, AX.X, ALU.min))
            nc.vector.tensor_copy(carry[:, 1, :], carry_in[:, 0:1].broadcast_to([P, HEADS])).then_inc(carry_ready, 1)
            dve.wait_ge(carryT, 1)
            nc.vector.tensor_copy(carry_row[:, 0, 0:P], tps[0:HEADS, 0, 0:P])
            nc.vector.memset(carry_row[:, 2, 0:1], NEG)
            link(nc.vector.tensor_copy(carry_row[:, 1, 0:P], tps[0:HEADS, 1, 0:P]))
            nc.vector.tensor_tensor_scan(carry_row[:, 2, 1:P + 1], carry_row[:, 1, 0:P], carry_row[:, 0, 0:P], NEG, ALU.add, ALU.max).then_inc(carry_done, 1)
            dve.wait_ge(carry_back, 1)
            link(nc.vector.tensor_copy(carry_in[:], dps[:, 0, 0:HEADS]))
            for hd in range(HEADS):
                last = nc.vector.tensor_tensor_scan(runmax[:, :, hd], fresh, s2e[:, :, hd], carry_in[:, hd:hd + 1], ALU.add, ALU.max)
            last.then_inc(runmax_ready, 1)
            link(nc.vector.memset(ACC[:], 0.0))
            dve.wait_ge(nbr_in, 16 * NT)
            link(nc.vector.tensor_tensor(nbr_max, nbr_max, node_sc[:, 0:NT, 0, :], ALU.add))
            nc.vector.scalar_tensor_tensor(node_sc[:, 0:NT, 1, :], nbr_max, 0.2, nbr_max, ALU.mult, ALU.max).then_inc(sc_ready, 1)
            with dve.Fori(0, BODIES) as i:
                for h in range(RING):
                    j = i * RING + h
                    group = rows[:, h * GROUP:(h + 1) * GROUP, :]
                    es = dps[:, 1, 0:GROUP * 2 * HEADS].rearrange("p (g t a) -> p g t a", g=GROUP, t=2)
                    dve.wait_ge(edge_sc, j + 1)
                    dve.wait_ge(rows_landed[h], (i + 1) * (16 * GROUP))
                    nc.vector.tensor_tensor(zs[:, 0, :, :], es[:, :, 0, :], group[:, :, D:HD], ALU.add).then_inc(act_step, 1)
                    dve.wait_ge(act_step, j * 2 + 1)
                    nc.vector.scalar_tensor_tensor(zs[:, 1, :, :], zs[:, 0, :, :], 0.2, zs[:, 0, :, :], ALU.mult, ALU.max).then_inc(act_step, 1)
                    dve.wait_ge(act_step, j * 2 + 2)
                    nc.vector.tensor_tensor(zs[:, 2, :, :], es[:, :, 1, :], zs[:, 1, :, :], ALU.subtract).then_inc(z_ready, 1)
                    make_onehot((Q_ATT * BODIES + i) * RING + h + 1, (j + 1) * GROUP, (h + 1) % 2)
                    dve.wait_ge(p_ready, j + 1)
                    hh = group[:, :, 0:D].rearrange("p g (a o) -> p g a o", a=HEADS)
                    nc.vector.tensor_tensor(hh, hh, group[:, :, D:HD].unsqueeze(3).broadcast_to([P, GROUP, HEADS, DH]), ALU.mult).then_inc(weighted, 1)
                    add_steps(Q_ATT, i, h, lambda n: ACC[:, bass.ds(n, 1), :], HD)
            link(nc.vector.tensor_scalar(rden, ACC[:, 0:NT, D:HD], 1e-30, None, ALU.max))
            link(nc.vector.reciprocal(rden, rden))
            a4v = ACC[:, 0:NT, 0:D].rearrange("p n (a o) -> p n a o", a=HEADS)
            link(nc.vector.tensor_tensor(a4v, a4v, rden.unsqueeze(3).broadcast_to([P, NT, HEADS, DH]), ALU.mult))
            nc.vector.scalar_tensor_tensor(res3, ACC[:, 0:NT, 0:D], 0.0, X[:], ALU.max, ALU.add).then_inc(acc_free, 1)
            dve.wait_ge(acc_free, 1)
            layernorm(res3)
            layernorm_end(3)
            with dve.Fori(0, NB) as i:
                dve.wait_ge(y_batch, i + 1)
                dve.nop(nofuse=True)
                for u in range(U):
                    n = i * U + u
                    dve.wait_ge(x0_ready, n + 1)
                    nc.vector.tensor_scalar(ybuf[:, u, 0:D], X[:, bass.ds(n, 1), :], dinv[:, bass.ds(n, 1)], None, ALU.mult).then_inc(y_ready, 1)
            dve.engine_nop().then_inc(g_x, 2)
            with dve.Fori(1, LAYERS + 1) as k:
                dve.wait_ge(acc_clear, (k - 1) * NT + 1)
                dve.nop(nofuse=True)
                with dve.Fori(0, BODIES) as i:
                    for h in range(RING):
                        make_onehot(((Q_LAYER - 1 + k) * BODIES + i) * RING + h + 1, (i * RING + h + 1) * GROUP, (h + 1) % 2)
                        add_steps(Q_LAYER - 1 + k, i, h, lambda n: ACC[:, bass.ds(n, 1), 0:D], D)
                dve.engine_nop().then_inc(passes_added, 1)
                dve.wait_ge(z_done, k * NT)
                dve.nop(nofuse=True)
                with dve.Fori(0, NB) as i:
                    dve.wait_ge(y_batch, k * NB + i + 1)
                    dve.nop(nofuse=True)
                    for u in range(U):
                        n = i * U + u
                        m = (k - 1) * NT + n
                        dve.wait_ge(g_ps, m + 3)
                        nc.vector.tensor_tensor(X[:, bass.ds(n, 1), :], X[:, bass.ds(n, 1), :], dps[:, u % 2, 0:D], ALU.add).then_inc(g_x, 1)
                        dve.wait_ge(g_x, m + 3)
                        nc.vector.tensor_scalar(ybuf[:, u, 0:D], X[:, bass.ds(n, 1), :], dinv[:, bass.ds(n, 1)], None, ALU.mult).then_inc(y_ready, 1)
            dve.wait_ge(y_ready, (LAYERS + 1) * NT)
            for c in range(U):
                t = slice(c * NB, (c + 1) * NB)
                nc.vector.tensor_tensor(X[:, t, :], X[:, t, :], res3[:, t, :], ALU.add).then_inc(out_ready, 1)

        @block.tensor
        def _(pe):
            for sem, credit in ((h_tr, 2), (proj_ready, 2), (g_tr, 2), (g_ps, 2), (step_summed, CREDIT)):
                pe.nop(nofuse=True).then_inc(sem, credit)
            pe.wait_ge(cmp_ready, 1)
            for ic in range(SC):
                for c in range(SC):
                    nc.tensor.matmul(dps[:, 0, ic:ic + 1], cmp[:, c, ic * P:(ic + 1) * P], ones_b[:], start=(c == 0), stop=(c == SC - 1))
            HS = SPAD // 2
            for b in range(2):
                for c in range(SC):
                    last = nc.tensor.matmul(tps[0:1, b, 0:HS], ones_b[:], cmp[:, c, b * HS:(b + 1) * HS], start=(c == 0), stop=(c == SC - 1))
            last.then_inc(counts_ready, 1)
            pe.wait_ge(steps_f, 1)
            for b in range(2):
                for c in range(4 * b, min(SC, 4 * b + 4)):
                    o = (c - 4 * b) * P
                    nc.tensor.transpose(agg[:, b, o:o + P], drowf[:, c, :], ident[:])
                    last = nc.tensor.transpose(agg[:, 2 + b, o:o + P], srowf[:, c, :], ident[:])
            last.then_inc(stepsT, 1)
            pe.wait_ge(wext_ready, 1)
            with pe.Fori(0, NB) as i:
                def turn(u):
                    n = i * U + u
                    pe.wait_ge(h_ready, n + 1)
                    pe.wait_ge(hT_ready, n + (2 if u == 0 else 1))
                    for c in range(2):
                        last = nc.tensor.transpose(tps[:, u % 2, c * P:(c + 1) * P], tileS[:, u % 2, c * P:(c + 1) * P], ident[:])
                    last.then_inc(h_tr, 1)

                turn(0)
                for u in range(U):
                    n = i * U + u
                    if u + 1 < U:
                        turn(u + 1)
                    pe.wait_ge(hT_ready, n + 3)
                    pe.wait_ge(proj_copied, n + (2 if u == 0 else 1))
                    for c in range(2):
                        last = nc.tensor.matmul(dps[:, u % 2, 0:PX], tileT[:, u % 2, c, :], wA[:, c, :], start=(c == 0), stop=(c == 1))
                    last.then_inc(proj_ready, 1)

            def sum_step(J, h, s, rhs, width):
                pe.wait_ge(step_added, J * GROUP + s + 1)
                nc.tensor.matmul(agg[:, s, 0:width], onehot[:, h % 2, s, :], rhs, start=True, stop=True).then_inc(step_summed, 1)

            with pe.Fori(0, BODIES) as i:
                for h in range(RING):
                    J = (Q_DEG * BODIES + i) * RING + h
                    pe.wait_ge(onehot_ready, J + 1)
                    for s in range(GROUP):
                        sum_step(J, h, s, ones[:, 0:1], 1)
            pe.wait_ge(deg_ready, 1)
            nc.tensor.matmul(dps[:, 0, 0:NT], tri, degree[:, 0:NT], start=True, stop=True)
            nc.tensor.matmul(dps[:, 1, 0:NT], ones[:], degree[:, 0:NT], start=True, stop=True).then_inc(cum_ready, 1)
            pe.wait_ge(carry_ready, 1)
            nc.tensor.transpose(tps[0:HEADS, 0, 0:P], carry[:, 0, :], ident[:])
            nc.tensor.transpose(tps[0:HEADS, 1, 0:P], carry[:, 1, :], ident[:]).then_inc(carryT, 1)
            pe.wait_ge(carry_done, 1)
            nc.tensor.transpose(dps[:, 0, 0:HEADS], carry_row[:, 2, 0:P], ident[0:HEADS, 0:HEADS]).then_inc(carry_back, 1)

            def transpose_onehots(j, h):
                pe.wait_ge(onehot_ready, Q_ATT * GROUPS + j + 1)
                for s in range(GROUP):
                    last = nc.tensor.transpose(tps[:, 0, s * P:(s + 1) * P], onehot[:, h % 2, s, :], ident[:])
                last.then_inc(ohT_ps, 1)

            def edge_scores(j):
                tiles = step_tiles(mybir.EngineType.PE, j)
                pe.wait_ge(ohT_ready, j + 1)
                for s, n in enumerate(tiles):
                    last = nc.tensor.matmul(dps[:, 1, s * 2 * HEADS:(s + 1) * 2 * HEADS], onehotT[:, s, :],
                                            node_sc[:, bass.ds(n, 1), :, :].rearrange("p n t a -> p (n t a)"), start=True, stop=True)
                last.then_inc(edge_sc, 1)

            pe.wait_ge(sc_ready, 1)
            transpose_onehots(0, 0)
            edge_scores(0)
            with pe.Fori(0, BODIES) as i:
                for h in range(RING):
                    j = i * RING + h
                    transpose_onehots(j + 1, h + 1)
                    edge_scores(j + 1)
                    pe.wait_ge(weighted, j + 1)
                    for s in range(GROUP):
                        sum_step(Q_ATT * GROUPS + j, h, s, rows[:, h * GROUP + s, :], HD)
            with pe.Fori(1, LAYERS + 1) as k:
                pe.wait_ge(w_layer, 32 * k)
                pe.nop(nofuse=True)

                def body(i, dense):
                    for h in range(RING):
                        J = ((Q_LAYER - 1 + k) * BODIES + i) * RING + h
                        m = (k - 1) * NT + i
                        pe.wait_ge(onehot_ready, J + 1)
                        pe.wait_ge(rows_landed[h], (k * BODIES + i + 1) * (16 * GROUP))
                        for s in range(GROUP):
                            sum_step(J, h, s, rows[:, h * GROUP + s, 0:D], D)
                        if dense and h == 1:
                            pe.wait_ge(z_copy, m + 1)
                            for c in range(2):
                                last = nc.tensor.transpose(tps[:, 0, c * P:(c + 1) * P], tileS[:, 0, c * P:(c + 1) * P], ident[:])
                            last.then_inc(z_tr, 1)
                        if dense and h == 2:
                            pe.wait_ge(z_copyT, m + 1)
                            for c in range(2):
                                last = nc.tensor.matmul(dps[:, 0, 0:D], tileT[:, 0, c, :], wA[:, c, 0:D], start=(c == 0), stop=(c == 1))
                            last.then_inc(z_ps, 1)

                with pe.Fori(0, NT) as i:
                    body(i, True)
                with pe.Fori(NT, BODIES) as i:
                    body(i, False)
                with pe.Fori(0, NB) as i:
                    def turn(u):
                        m = (k - 1) * NT + i * U + u
                        pe.wait_ge(g_copy, m + 1)
                        pe.wait_ge(g_copyT, m + (2 if u == 0 else 1))
                        for c in range(2):
                            last = nc.tensor.transpose(tps[:, u % 2, c * P:(c + 1) * P], tileS[:, u % 2, c * P:(c + 1) * P], ident[:])
                        last.then_inc(g_tr, 1)

                    turn(0)
                    for u in range(U):
                        m = (k - 1) * NT + i * U + u
                        if u + 1 < U:
                            turn(u + 1)
                        pe.wait_ge(g_copyT, m + 3)
                        pe.wait_ge(g_x, m + (2 if u == 0 else 1))
                        for c in range(2):
                            last = nc.tensor.matmul(dps[:, u % 2, 0:D], tileT[:, u % 2, c, :], wB[:, c, :], start=(c == 0), stop=(c == 1))
                        last.then_inc(g_ps, 1)


def kernel(x, src, dst, L0_gnn_W, L0_gnn_a, L1_gnn_W0, L1_gnn_W1):
    import numpy as np
    import concourse.bacc as bacc
    from concourse.bass_utils import run_bass_kernel_spmd

    nc = bacc.Bacc("TRN2", target_bir_lowering=False, num_devices=1)
    laid_out = {
        "x": np.asarray(x), "src": np.asarray(src), "dst": np.asarray(dst),
        "w_att": np.asarray(L0_gnn_W).transpose(1, 0, 2).reshape(D, HEADS * DH), "a_att": np.asarray(L0_gnn_a),
        "w0t": np.asarray(L1_gnn_W0).transpose(0, 2, 1), "w1t": np.asarray(L1_gnn_W1).transpose(0, 2, 1),
    }
    arrays, args = {}, []
    for name, a in laid_out.items():
        a = np.ascontiguousarray(a)
        arrays["in_" + name] = a
        args.append(nc.dram_tensor("in_" + name, a.shape, mybir.dt.from_np(a.dtype), kind="ExternalInput").ap())
    args.append(nc.dram_tensor("out_0", (N, D), F32, kind="ExternalOutput").ap())
    program(nc, *args)
    r = run_bass_kernel_spmd(nc, [arrays], core_ids=[0])
    return r.results[0]["out_0"]
```

```python
import concourse.bass as bass
from concourse import mybir

F32 = mybir.dt.float32
BF16 = mybir.dt.bfloat16
I32 = mybir.dt.int32
ALU = mybir.AluOpType
ACT = mybir.ActivationFunctionType
AX = mybir.AxisListType

P = 128
N, D = 6250, 256
HEADS, DH = 4, 64
E = 106250
LAYERS = 5
EPS = 1e-5
NT = -(-N // P)
LAST = N - (NT - 1) * P
ET = -(-E // P)
GROUP = 4
RING = 4
BODY = GROUP * RING
BODIES = -(-(ET + NT - 1) // BODY)
STEPS = BODIES * BODY
GROUPS = STEPS // GROUP
SC = -(-STEPS // P)
SPAD = SC * P
PER = 832
ROWS = PER
U = 7
NB = NT // U
HD = D + HEADS
PX = HD + HEADS
SU = 8
SGROUPS = PER // SU
FAR = 100000
NEG = -1e30
FULL, PART = (ET - 1) // P * P, (ET - 1) % P
REST = E - (ET - 1) * P
CREDIT = 4


def program(nc, x, src, dst, w_att, a_att, w0t, w1t, out):
    def sb(name, shape, dt=F32):
        return nc.alloc_sbuf_tensor(name, shape, dt)

    def dram(name, shape, dt=F32):
        return nc.dram_tensor(name, shape, dt, kind="Internal").ap()

    src_rows = dram("src_rows", (ROWS + 1, P), I32)
    dst_rows = dram("dst_rows", (ROWS + 1, P), I32)
    att_table = dram("att_table", (NT * P, D))
    s2_table = dram("s2_table", (NT * P, HEADS))
    runmax_table = dram("runmax_table", (P * PER, HEADS))
    run_table = dram("run_table", (P * PER + NT * P, 2 * HEADS))
    p_table = dram("p_table", (ROWS, P * HEADS))
    y_table = dram("y_table", (NT * P, D))

    X = sb("X", [P, NT, D])
    RES = sb("RES", [P, NT * D])
    ACC = sb("ACC", [P, NT + 1, HD])
    rows = sb("rows", [P, BODY, HD])
    onehot = sb("onehot", [P, 2, GROUP, P])
    loc = sb("loc", [P, SPAD])
    gidx = sb("gidx", [P, SPAD], I32)
    gidx_now = sb("gidx_now", [P, RING, GROUP], I32)
    ntile = sb("ntile", [1, STEPS + GROUP], I32)
    wA = sb("wA", [P, 2, PX])
    wB = sb("wB", [P, 2, D])
    ybuf = sb("ybuf", [P, U, HD])
    tileS = sb("tileS", [P, 2, D])
    tileT = sb("tileT", [P, 2, 2, P])
    iota_free = sb("iota_free", [P, P])
    ident = sb("ident", [P, P])
    ones = sb("ones", [P, P])
    ones_b = sb("ones_b", [P, 1], BF16)
    zero = sb("zero", [P, 1])
    chunk_id = sb("chunk_id", [P, SC])
    small = sb("small", [P, 12, SC])
    small_i = sb("small_i", [P, 2, SC], I32)
    header = sb("header", [1, P], I32)
    degree = sb("degree", [P, NT + 1])
    dinv = sb("dinv", [P, NT])
    meanvar = sb("meanvar", [P, NT, 2])
    rstd = sb("rstd", [P, NT])
    shift = sb("shift", [P, NT])
    last_edge = sb("last_edge", [P, NT], I32)
    node_sc = sb("node_sc", [P, NT + 1, 2, HEADS])
    carry = sb("carry", [P, 2, 2 * HEADS])
    carry_row = sb("carry_row", [2 * HEADS, 3, P + 1])
    carry_in = sb("carry_in", [P, 2 * HEADS])
    node_id = sb("node_id", [P, NT])
    first_edge = sb("first_edge", [P, NT], I32)

    accf = ACC[:].rearrange("p n f -> p (n f)")
    at = [0]

    def tmp(words):
        at[0] += words
        return accf[:, at[0] - words:at[0]]

    cmp = tmp(SC * SPAD // 2).bitcast(BF16).rearrange("p (c i) -> p c i", c=SC)
    srow = tmp(SPAD).bitcast(I32).rearrange("p (c e) -> p c e", c=SC)
    drow = tmp(SPAD).bitcast(I32).rearrange("p (c e) -> p c e", c=SC)
    srowf = tmp(SPAD).rearrange("p (c e) -> p c e", c=SC)
    drowf = tmp(SPAD).rearrange("p (c e) -> p c e", c=SC)
    iota_steps = tmp(SPAD)
    nrowf = tmp(SPAD)
    dchk = tmp(SPAD).bitcast(I32).rearrange("p (c e) -> p c e", c=SC)
    schk = tmp(SPAD).bitcast(I32).rearrange("p (c e) -> p c e", c=SC)
    a_bc = tmp(HEADS * 2 * DH)
    prod = tmp(D)
    s2e = RES[:, 0:PER * HEADS].rearrange("p (j h) -> p j h", h=HEADS)
    runmax = RES[:, PER * HEADS:2 * PER * HEADS].rearrange("p (j h) -> p j h", h=HEADS)
    o = 2 * PER * HEADS
    fresh = RES[:, o:o + PER]
    o += PER
    sidx = RES[:, o:o + PER + 2 * SU].bitcast(I32)
    o += PER + 2 * SU
    dcur = RES[:, o:o + PER].bitcast(I32)
    keep = RES[:, o:o + PER]
    dprev = RES[:, o + PER:o + 2 * PER].bitcast(I32)
    carried = RES[:, o + PER:o + 2 * PER]
    prow = RES[:, SPAD * HEADS:2 * SPAD * HEADS].rearrange("p (c e h) -> p c e h", c=SC, h=HEADS)
    pstep = RES[:, 0:SPAD * HEADS].rearrange("p (i h) -> p i h", h=HEADS)
    run = accf[:, 0:PER * 2 * HEADS].rearrange("p (j h) -> p j h", h=2 * HEADS)
    o += 2 * PER

    def rest(words):
        nonlocal o
        o += words
        return RES[:, o - words:o]

    tri = rest(P)
    cum = rest(3 * NT).rearrange("p (k n) -> p k n", k=3)
    nbr_max = rest(NT * HEADS).rearrange("p (n h) -> p n h", h=HEADS)
    rden = rest(NT * HEADS).rearrange("p (n h) -> p n h", h=HEADS)
    s2_rows = rest(2 * SU * HEADS).rearrange("p (b u h) -> p b u h", b=2, u=SU)
    s2_idx = rest(2 * SU).bitcast(I32).rearrange("p (b u) -> p b u", b=2)
    stats = ybuf[:].rearrange("p u f -> p (u f)")[:, 0:NT * 6].rearrange("p (n k) -> p n k", k=6)
    res3 = RES[:].rearrange("p (n f) -> p n f", f=D)

    agg = nc.alloc_psum_tensor("agg", [P, GROUP, 512], F32)
    tps = nc.alloc_psum_tensor("tps", [P, 2, 512], F32)
    dps = nc.alloc_psum_tensor("dps", [P, 2, 512], F32)

    S = nc.alloc_semaphore
    cleared, consts = S("cleared"), S("consts")
    edge_in, x_in, w_in, a_in, rows_out, lay_in = S("edge_in"), S("x_in"), S("w_in"), S("a_in"), S("rows_out"), S("lay_in")
    dve_step, act_step, pool_step = S("dve_step"), S("act_step"), S("pool_step")
    cmp_ready, counts_ready, tidx_ready, steps_in, steps_f, stepsT = (
        S("cmp_ready"), S("counts_ready"), S("tidx_ready"), S("steps_in"), S("steps_f"), S("stepsT"))
    plan_ready = S("plan_ready")
    wext_ready = S("wext_ready")
    var_ready, std_ready, norm_ready = S("var_ready"), S("std_ready"), S("norm_ready")
    h_ready, h_tr, hT_ready, proj_ready, proj_copied, att_sent, batch_out, table1 = (
        S("h_ready"), S("h_tr"), S("hT_ready"), S("proj_ready"), S("proj_copied"), S("att_sent"), S("batch_out"), S("table1"))
    s2idx_ready, s2_saved = S("s2idx_ready"), S("s2_saved")
    s2_landed = [S("s2_landed0"), S("s2_landed1")]
    fresh_ready = S("fresh_ready")
    onehot_ready, step_summed, step_added = S("onehot_ready"), S("step_summed"), S("step_added")
    idx_ready = S("idx_ready")
    rows_landed = [S(f"rows_landed{h}") for h in range(RING)]
    deg_ready, cum_ready, pos_ready = S("deg_ready"), S("cum_ready"), S("pos_ready")
    carry_ready, carryT, carry_done, carry_back = S("carry_ready"), S("carryT"), S("carry_done"), S("carry_back")
    runmax_ready, runmax_out, nbr_in, sc_ready = S("runmax_ready"), S("runmax_out"), S("nbr_in"), S("sc_ready")
    zeros_ready, zeros_out, values_out, run_in = S("zeros_ready"), S("zeros_out"), S("values_out"), S("run_in")
    p_ready, p_out, prow_in, prowT, pstep_ready, p_placed, weighted = (
        S("p_ready"), S("p_out"), S("prow_in"), S("prowT"), S("pstep_ready"), S("p_placed"), S("weighted"))
    gap_ready = S("gap_ready")
    acc_free, acc_clear, res_ready = S("acc_free"), S("acc_clear"), S("res_ready")
    x0_ready, y_ready, y_sent, y_batch = S("x0_ready"), S("y_ready"), S("y_sent"), S("y_batch")
    table_ready = S("table_ready")
    w_layer = S("w_layer")
    z_copy, z_tr, z_copyT, z_ps, z_done = S("z_copy"), S("z_tr"), S("z_copyT"), S("z_ps"), S("z_done")
    passes_added = S("passes_added")
    g_copy, g_tr, g_copyT, g_ps, g_x = S("g_copy"), S("g_tr"), S("g_copyT"), S("g_ps"), S("g_x")
    out_ready, out_sent = S("out_ready"), S("out_sent")

    Q_DEG, Q_ATT, Q_LAYER = 0, 1, 2

    def step_tiles(engine, group):
        _, tiles = nc.values_load_multi_w_load_instructions(ntile[0:1, bass.ds(group * GROUP, GROUP)], engines=(engine,),
                                                            min_val=0, max_val=NT)
        return tiles

    with nc.Block() as block:

        @block.sync
        def _(sp):
            sp.nop(nofuse=True).then_inc(batch_out, 1)
            sp.nop(nofuse=True).then_inc(y_batch, 1)
            sp.wait_ge(cleared, 1)
            for v, chk in ((dst, dchk), (src, schk)):
                sp.dma_start(chk[:, 0:SC - 1, :], v[0:FULL * P].rearrange("(c p e) -> p c e", p=P, e=P)).then_inc(edge_in, 16)
                sp.dma_start(chk[0:PART, SC - 1, :], v[FULL * P:(FULL + PART) * P].rearrange("(p e) -> p e", e=P)).then_inc(edge_in, 16)
                sp.dma_start(chk[PART:PART + 1, SC - 1, 0:REST], v[(ET - 1) * P:E].rearrange("(p e) -> p e", p=1)).then_inc(edge_in, 16)
            sp.wait_ge(edge_in, 96)
            for r, chk in ((dst_rows, dchk), (src_rows, schk)):
                sp.dma_start(r[1:1 + FULL, :].rearrange("(c p) e -> p c e", p=P), chk[:, 0:SC - 1, :]).then_inc(rows_out, 16)
                sp.dma_start(r[1 + FULL:1 + ROWS, :], chk[0:ROWS - FULL, SC - 1, :]).then_inc(rows_out, 16)
                sp.dma_start(r[0:1, :], header[:]).then_inc(rows_out, 16)
            sp.dma_start(X[:, 0:NT - 1, :], x[0:(NT - 1) * P, :].rearrange("(n p) f -> p n f", p=P)).then_inc(x_in, 16)
            sp.dma_start(X[0:LAST, NT - 1, :], x[(NT - 1) * P:N, :]).then_inc(x_in, 16)
            sp.dma_start(wA[:, :, 0:D], w_att.rearrange("(c p) f -> p c f", p=P)).then_inc(w_in, 16)
            sp.dma_start(a_bc, a_att.rearrange("h o -> (h o)").partition_broadcast(P)).then_inc(a_in, 16)
            sp.wait_ge(rows_out, 96)
            sflat = src_rows.rearrange("r e -> (r e)")
            dflat = dst_rows.rearrange("r e -> (r e)")
            sp.dma_start(sidx[:, 0:PER], sflat[P:P + P * PER].rearrange("(p j) -> p j", p=P)).then_inc(lay_in, 16)
            sp.dma_start(dcur, dflat[P:P + P * PER].rearrange("(p j) -> p j", p=P)).then_inc(lay_in, 16)
            sp.dma_start(dprev, dflat[P - 1:P - 1 + P * PER].rearrange("(p j) -> p j", p=P)).then_inc(lay_in, 16)
            with sp.Fori(0, NB) as i:
                for u in range(U):
                    sp.wait_ge(proj_copied, i * U + u + 1 + 2)
                    sp.dma_start(att_table[bass.ds((i * U + u) * P, P), :], ybuf[:, u, 0:D]).then_inc(att_sent, 16)
                    sp.dma_start(s2_table[bass.ds((i * U + u) * P, P), :], ybuf[:, u, D:HD]).then_inc(att_sent, 16)
                sp.wait_ge(att_sent, (i + 1) * (U * 32))
                sp.nop(nofuse=True).then_inc(batch_out, 1)
            sp.wait_ge(zeros_ready, 1)
            sp.dma_start(run_table[0:P * PER, :].rearrange("(p j) h -> p (j h)", p=P), accf[:, 0:PER * 2 * HEADS]).then_inc(zeros_out, 16)
            sp.wait_ge(runmax_ready, 1)
            sp.dma_start(runmax_table.rearrange("(p j) h -> p j h", p=P), runmax).then_inc(runmax_out, 16)
            sp.wait_ge(values_out, 16 * NT)
            sp.dma_start(run, run_table[0:P * PER, :].rearrange("(p j) h -> p j h", p=P)).then_inc(run_in, 16)
            sp.wait_ge(p_ready, 1)
            sp.dma_start(p_table.rearrange("r (e h) -> (r e) h", h=HEADS).rearrange("(p j) h -> p j h", p=P), s2e).then_inc(p_out, 16)
            sp.dma_start(wB[:], w1t[0:1].rearrange("l (c p) f -> p (l c) f", p=P)).then_inc(w_layer, 16)
            sp.wait_ge(proj_ready, NT + 2)
            sp.dma_start(wA[:, :, 0:D], w0t[0:1].rearrange("l (c p) f -> p (l c) f", p=P)).then_inc(w_layer, 16)

            def send_y(k):
                with sp.Fori(0, NB) as i:
                    for u in range(U):
                        sp.wait_ge(y_ready, k * NT + i * U + u + 1)
                        sp.dma_start(y_table[bass.ds((i * U + u) * P, P), :], ybuf[:, u, 0:D]).then_inc(y_sent, 16)
                    sp.wait_ge(y_sent, (k * NB + i + 1) * (U * 16))
                    sp.nop(nofuse=True).then_inc(y_batch, 1)

            send_y(0)
            with sp.Fori(1, LAYERS) as k:
                send_y(k)
                sp.wait_ge(g_ps, k * NT + 2)
                sp.dma_start(wA[:, :, 0:D], w0t[bass.ds(k, 1)].rearrange("l (c p) f -> p (l c) f", p=P)).then_inc(w_layer, 16)
                sp.dma_start(wB[:], w1t[bass.ds(k, 1)].rearrange("l (c p) f -> p (l c) f", p=P)).then_inc(w_layer, 16)
            send_y(LAYERS)
            for c in range(U):
                sp.wait_ge(out_ready, c + 1)
                t0, t1 = c * NB, (c + 1) * NB
                if c < U - 1:
                    sp.dma_start(out[t0 * P:t1 * P, :].rearrange("(n p) f -> p n f", p=P), X[:, t0:t1, :]).then_inc(out_sent, 16)
                else:
                    sp.dma_start(out[t0 * P:(NT - 1) * P, :].rearrange("(n p) f -> p n f", p=P), X[:, t0:NT - 1, :]).then_inc(out_sent, 16)
                    sp.dma_start(out[(NT - 1) * P:N, :], X[0:LAST, NT - 1, :]).then_inc(out_sent, 16)
            sp.wait_ge(out_sent, 16 * (U + 1))

        @block.gpsimd
        def _(pool):
            pool.iota(iota_free[:], [[1, P]], base=0, channel_multiplier=0, allow_small_or_imprecise_dtypes=True)
            pool.iota(iota_steps, [[1, SPAD]], base=0, channel_multiplier=0, allow_small_or_imprecise_dtypes=True)
            pool.iota(chunk_id[:], [[P, SC]], base=0, channel_multiplier=1, allow_small_or_imprecise_dtypes=True)
            pool.iota(node_id[:], [[P, NT]], base=0, channel_multiplier=1, allow_small_or_imprecise_dtypes=True)
            pool.memset(ident[:], 0.0)
            pool.memset(tri, 1.0).then_inc(pool_step, 1)
            pool.wait_ge(pool_step, 1)
            pool.affine_select(out=ident[:], in_=ident[:], compare_op=ALU.not_equal, fill=1.0, base=0,
                               pattern=[[-1, P]], channel_multiplier=1)
            pool.affine_select(out=tri, in_=tri, compare_op=ALU.is_ge, fill=0.0, base=0,
                               pattern=[[1, P]], channel_multiplier=-1).then_inc(consts, 1)
            pool.wait_ge(rows_out, 96)
            pool.wait_ge(tidx_ready, 1)
            for c in range(SC):
                at_c = bass.IndirectOffsetOnAxis(ap=small_i[:, 1, c:c + 1], axis=0)
                pool.indirect_dma_start(srow[:, c, :], None, src_rows, at_c).then_inc(steps_in, 16)
                pool.indirect_dma_start(drow[:, c, :], None, dst_rows, at_c).then_inc(steps_in, 16)
            pool.wait_ge(batch_out, NB + 1)
            with pool.Fori(0, SGROUPS // 2) as i:
                for h in range(2):
                    pool.wait_ge(s2idx_ready, 2 * i + h + 1)
                    pool.nop(nofuse=True)
                    for u in range(SU):
                        pool.indirect_dma_start(s2_rows[:, h, u, :], None, s2_table,
                                                bass.IndirectOffsetOnAxis(ap=s2_idx[:, h, u:u + 1], axis=0)).then_inc(s2_landed[h], 16)
            pool.wait_ge(runmax_out, 16)
            pool.wait_ge(pos_ready, 1)
            for n in range(NT):
                pool.indirect_dma_start(nbr_max[:, n, :], None, runmax_table,
                                        bass.IndirectOffsetOnAxis(ap=last_edge[:, n:n + 1], axis=0)).then_inc(nbr_in, 16)

            def gather(q, table, width):
                with pool.Fori(0, BODIES) as i:
                    for h in range(RING):
                        pool.wait_ge(idx_ready, (q * BODIES + i) * RING + h + 1)
                        pool.nop(nofuse=True)
                        for u in range(GROUP):
                            pool.indirect_dma_start(rows[:, h * GROUP + u, 0:width], None, table,
                                                    bass.IndirectOffsetOnAxis(ap=gidx_now[:, h, u:u + 1], axis=0)).then_inc(rows_landed[h], 16)

            pool.wait_ge(sc_ready, 1)
            pool.wait_ge(zeros_out, 16)
            for n in range(NT):
                pool.indirect_dma_start(run_table, bass.IndirectOffsetOnAxis(ap=first_edge[:, n:n + 1], axis=0),
                                        node_sc[:, n, :, :].rearrange("p t a -> p (t a)"), None).then_inc(values_out, 16)
            pool.wait_ge(p_out, 16)
            for c in range(SC):
                pool.indirect_dma_start(prow[:, c, :, :].rearrange("p e h -> p (e h)"), None, p_table,
                                        bass.IndirectOffsetOnAxis(ap=small_i[:, 0, c:c + 1], axis=0)).then_inc(prow_in, 16)
            pool.memset(ACC[:], 0.0).then_inc(acc_clear, 1)
            gather(0, att_table, D)
            pool.wait_ge(acc_free, 1)
            pool.memset(ACC[:], 0.0).then_inc(acc_clear, 1)
            with pool.Fori(1, LAYERS + 1) as k:
                pool.wait_ge(y_batch, k * NB + 1)
                pool.nop(nofuse=True)
                gather(k, y_table, D)
                with pool.Fori(0, NT) as n:
                    pool.wait_ge(g_copy, (k - 1) * NT + n + 1)
                    pool.nop(nofuse=True)
                    pool.tensor_copy(ACC[:, bass.ds(n, 1), 0:D], zero[:, 0:1].unsqueeze(2).broadcast_to([P, 1, D])).then_inc(acc_clear, 1)

        @block.scalar
        def _(act):
            act.nop(nofuse=True).then_inc(hT_ready, 2)
            act.nop(nofuse=True).then_inc(g_copyT, 2)
            act.wait_ge(var_ready, 1)
            act.activation(rstd[:], rstd[:], ACT.Sqrt).then_inc(std_ready, 1)
            act.wait_ge(norm_ready, 1)
            with act.Fori(0, NB) as i:
                def normalise(u):
                    n = i * U + u
                    act.wait_ge(h_tr, n + (2 if u == 0 else 1))
                    act.nop(nofuse=True)
                    act.activation(tileS[:, u % 2, :], X[:, bass.ds(n, 1), :], ACT.Relu, bias=shift[:, bass.ds(n, 1)],
                                   scale=rstd[:, bass.ds(n, 1)]).then_inc(h_ready, 1)

                normalise(0)
                for u in range(U):
                    n = i * U + u
                    if u + 1 < U:
                        normalise(u + 1)
                    act.wait_ge(h_tr, n + 3)
                    act.wait_ge(proj_ready, n + (2 if u == 0 else 1))
                    act.activation(tileT[:, u % 2, :, :], tps[:, u % 2, 0:D].rearrange("p (c m) -> p c m", c=2), ACT.Copy).then_inc(hT_ready, 1)
            act.wait_ge(lay_in, 48)
            for h in range(2):
                act.activation(s2_idx[:, h, :], sidx[:, h * SU:(h + 1) * SU], ACT.Copy).then_inc(s2idx_ready, 1)
            with act.Fori(0, SGROUPS // 2) as i:
                for h in range(2):
                    act.wait_ge(s2_landed[h], (i + 1) * (16 * SU))
                    act.nop(nofuse=True)
                    act.activation(s2e[:, bass.ds((2 * i + h) * SU, SU), :], s2_rows[:, h, :, :], ACT.Copy).then_inc(s2_saved, 1)
                    act.activation(s2_idx[:, h, :], sidx[:, bass.ds((2 * i + h + 2) * SU, SU)], ACT.Copy).then_inc(s2idx_ready, 1)
            act.wait_ge(plan_ready, 1)
            act.activation(dinv[:], cum[:, 2, :], ACT.Sqrt).then_inc(std_ready, 1)
            for h in range(RING):
                act.activation(gidx_now[:, h, :], gidx[:, h * GROUP:(h + 1) * GROUP], ACT.Copy).then_inc(idx_ready, 1)

            def next_index(q, i, h):
                act.wait_ge(step_summed, ((q * BODIES + i) * RING + h + 1) * GROUP + CREDIT)
                act.nop(nofuse=True)
                act.activation(gidx_now[:, h, :], gidx[:, bass.ds((i * RING + h + RING) * GROUP, GROUP)], ACT.Copy).then_inc(idx_ready, 1)

            act.wait_ge(gap_ready, 1)
            act.activation(s2e, s2e, ACT.Exp).then_inc(p_ready, 1)
            for c in range(SC):
                act.wait_ge(prowT, c + 1)
                act.activation(pstep[:, c * P:(c + 1) * P, :], agg[:, c % GROUP, :].rearrange("p (h i) -> p i h", h=HEADS), ACT.Copy).then_inc(pstep_ready, 1)
            act.wait_ge(pstep_ready, SC)
            with act.Fori(0, BODIES) as i:
                for h in range(RING):
                    act.activation(rows[:, h * GROUP:(h + 1) * GROUP, D:HD], pstep[:, bass.ds((i * RING + h) * GROUP, GROUP), :], ACT.Copy).then_inc(p_placed, 1)
                    next_index(Q_ATT, i, h)
            act.wait_ge(var_ready, 2)
            act.activation(rstd[:], rstd[:], ACT.Sqrt).then_inc(std_ready, 1)
            act.wait_ge(norm_ready, 2)
            with act.Fori(0, NT) as n:
                act.activation(X[:, bass.ds(n, 1), :], res3[:, bass.ds(n, 1), :], ACT.Relu, bias=shift[:, bass.ds(n, 1)],
                               scale=rstd[:, bass.ds(n, 1)]).then_inc(x0_ready, 1)
            act.wait_ge(x0_ready, NT)
            with act.Fori(1, LAYERS + 1) as k:
                act.wait_ge(g_x, (k - 1) * NT + 2)
                act.nop(nofuse=True)

                def body(i, dense):
                    for h in range(RING):
                        next_index(Q_LAYER - 1 + k, i, h)
                        m = k * NT - NT + i
                        if dense and h == 0:
                            act.activation(tileS[:, 0, :], X[:, bass.ds(i, 1), :], ACT.Copy).then_inc(z_copy, 1)
                        if dense and h == 1:
                            act.wait_ge(z_tr, m + 1)
                            act.activation(tileT[:, 0, :, :], tps[:, 0, 0:D].rearrange("p (c m) -> p c m", c=2), ACT.Copy).then_inc(z_copyT, 1)
                        if dense and h == 2:
                            act.wait_ge(z_ps, m + 1)
                            act.nop(nofuse=True)
                            act.activation(X[:, bass.ds(i, 1), :], dps[:, 0, 0:D], ACT.Copy).then_inc(z_done, 1)

                with act.Fori(0, NT) as i:
                    body(i, True)
                with act.Fori(NT, BODIES) as i:
                    body(i, False)
                act.wait_ge(passes_added, k)
                act.nop(nofuse=True)
                with act.Fori(0, NB) as i:
                    def scale_sums(u):
                        n = i * U + u
                        act.wait_ge(g_tr, (k - 1) * NT + n + (2 if u == 0 else 1))
                        act.nop(nofuse=True)
                        act.activation(tileS[:, u % 2, :], ACC[:, bass.ds(n, 1), 0:D], ACT.Copy, scale=dinv[:, bass.ds(n, 1)]).then_inc(g_copy, 1)

                    scale_sums(0)
                    for u in range(U):
                        m = (k - 1) * NT + i * U + u
                        if u + 1 < U:
                            scale_sums(u + 1)
                        act.wait_ge(g_tr, m + 3)
                        act.wait_ge(g_ps, m + (2 if u == 0 else 1))
                        act.activation(tileT[:, u % 2, :, :], tps[:, u % 2, 0:D].rearrange("p (c m) -> p c m", c=2), ACT.Copy).then_inc(g_copyT, 1)

        @block.vector
        def _(dve):
            links = [0]

            def link(ins):
                links[0] += 1
                ins.then_inc(dve_step, 1)
                dve.wait_ge(dve_step, links[0])

            nc.vector.memset(dchk[:, SC - 1, :], FAR)
            nc.vector.memset(schk[:, SC - 1, :], 0)
            nc.vector.memset(header[:], -1)
            nc.vector.memset(X[:, NT - 1, :], 0.0)
            nc.vector.memset(sidx[:, PER:PER + 2 * SU], 0)
            nc.vector.memset(ones[:], 1.0)
            nc.vector.memset(ones_b[:], 1.0)
            nc.vector.memset(zero[:], 0.0)
            nc.vector.memset(node_sc[:], 0.0)
            nc.vector.memset(degree[:], 0.0).then_inc(cleared, 1)
            dve.engine_nop().then_inc(proj_copied, 2)

            def layernorm(tiles):
                with dve.Fori(0, NT) as n:
                    nc.vector.bn_stats(stats[:, bass.ds(n, 1), :], tiles[:, bass.ds(n, 1), :])
                link(dve.engine_nop())
                mean, var = meanvar[:, :, 0], meanvar[:, :, 1]
                link(nc.vector.tensor_tensor(var, stats[:, :, 1], stats[:, :, 4], ALU.subtract))
                link(nc.vector.tensor_tensor(var, var, var, ALU.mult))
                link(nc.vector.tensor_scalar(var, var, 0.25, EPS, ALU.mult, ALU.add))
                link(nc.vector.tensor_tensor(mean, stats[:, :, 2], stats[:, :, 5], ALU.add))
                link(nc.vector.scalar_tensor_tensor(rstd[:], mean, 1.0 / D, var, ALU.mult, ALU.add))
                link(nc.vector.tensor_tensor(mean, stats[:, :, 1], stats[:, :, 4], ALU.add))
                nc.vector.tensor_scalar(mean, mean, 0.5, None, ALU.mult).then_inc(var_ready, 1)

            def layernorm_end(count):
                dve.wait_ge(std_ready, count)
                link(nc.vector.reciprocal(rstd[:], rstd[:]))
                link(nc.vector.tensor_tensor(shift[:], meanvar[:, :, 0], rstd[:], ALU.mult))
                nc.vector.tensor_scalar(shift[:], shift[:], -1.0, None, ALU.mult).then_inc(norm_ready, 1)

            dve.wait_ge(edge_in, 96)
            dve.wait_ge(consts, 1)
            link(nc.vector.tensor_single_scalar(small_i[:, 0, :], dchk[:, :, 0], 7, ALU.arith_shift_right))
            link(nc.vector.tensor_copy(small[:, 0, :], small_i[:, 0, :]))
            link(nc.vector.tensor_tensor(small[:, 1, :], small[:, 0, :], chunk_id[:], ALU.add))
            link(nc.vector.tensor_scalar(small[:, 2, :], chunk_id[:], 0.0, None, ALU.is_gt))
            link(nc.vector.tensor_tensor(small[:, 3, :], small[:, 1, :], small[:, 2, :], ALU.mult))
            for c in range(SC):
                last = nc.vector.tensor_scalar(cmp[:, c, :], iota_steps, small[:, 3, c:c + 1], None, ALU.is_ge)
            last.then_inc(cmp_ready, 1)
            dve.wait_ge(counts_ready, 1)
            link(nc.vector.tensor_copy(small[:, 4, :], dps[:, 0, 0:SC]))
            nc.vector.tensor_copy(small_i[:, 1, :], small[:, 4, :]).then_inc(tidx_ready, 1)
            nc.vector.tensor_scalar(small_i[:, 0, :], small[:, 4, :], -1.0, None, ALU.add)
            link(nc.vector.tensor_tensor(small[:, 5, :], chunk_id[:], small[:, 4, :], ALU.subtract))
            link(nc.vector.tensor_scalar(small[:, 6, :], small[:, 5, :], 1.0, -float(P), ALU.add, ALU.mult))
            HS = SPAD // 2
            for b in range(2):
                last = nc.vector.tensor_tensor(nrowf[0:1, b * HS:(b + 1) * HS], iota_steps[0:1, b * HS:(b + 1) * HS],
                                               tps[0:1, b, 0:HS], ALU.subtract)
            link(last)
            nc.vector.tensor_scalar(ntile[:, 0:STEPS], nrowf[0:1, 0:STEPS], 1.0, None, ALU.add)
            link(nc.vector.tensor_scalar(ntile[:, STEPS:STEPS + GROUP], nrowf[0:1, 0:GROUP], 1.0, None, ALU.add))
            dve.wait_ge(w_in, 16)
            dve.wait_ge(a_in, 16)
            a4 = a_bc.rearrange("p (h s o) -> p h s o", h=HEADS, s=2)
            pr = prod.rearrange("p (h o) -> p h o", h=HEADS)
            for c in range(2):
                for half, col in ((1, D), (0, HD)):
                    link(nc.vector.tensor_tensor(pr, wA[:, c, 0:D].rearrange("p (h o) -> p h o", h=HEADS), a4[:, :, half, :], ALU.mult))
                    link(nc.vector.tensor_reduce(wA[:, c, col:col + HEADS], pr, AX.X, ALU.add))
            dve.engine_nop().then_inc(wext_ready, 1)
            dve.wait_ge(x_in, 32)
            layernorm(X)
            layernorm_end(1)
            dve.wait_ge(steps_in, 16 * 2 * SC)
            nc.vector.tensor_copy(srowf, srow)
            link(nc.vector.tensor_copy(drowf, drow))
            for c in range(SC):
                last = nc.vector.tensor_scalar(drowf[:, c, :], drowf[:, c, :], small[:, 6, c:c + 1], None, ALU.add)
            last.then_inc(steps_f, 1)
            dve.wait_ge(stepsT, 1)
            for b in range(2):
                w = (min(SC, 4 * b + 4) - 4 * b) * P
                nc.vector.tensor_copy(loc[:, b * 512:b * 512 + w], agg[:, b, 0:w])
                last = nc.vector.tensor_copy(gidx[:, b * 512:b * 512 + w], agg[:, 2 + b, 0:w])
            link(last)
            nc.vector.tensor_copy(loc[:, STEPS:SPAD], loc[:, 0:SPAD - STEPS])
            link(nc.vector.tensor_copy(gidx[:, STEPS:SPAD], gidx[:, 0:SPAD - STEPS]))
            nc.vector.memset(accf[:, 0:PER * 2 * HEADS], 0.0).then_inc(zeros_ready, 1)
            dve.wait_ge(lay_in, 48)
            link(nc.vector.tensor_tensor(fresh, dcur, dprev, ALU.not_equal))
            link(nc.vector.tensor_scalar(fresh, fresh, NEG, None, ALU.mult))
            with dve.Fori(0, NB) as i:
                dve.wait_ge(batch_out, i + 1)
                dve.nop(nofuse=True)
                for u in range(U):
                    n = i * U + u
                    dve.wait_ge(proj_ready, n + 3)
                    nc.vector.tensor_copy(ybuf[:, u, :], dps[:, u % 2, 0:HD])
                    nc.vector.tensor_copy(node_sc[:, bass.ds(n, 1), 0, :], dps[:, u % 2, HD:PX]).then_inc(proj_copied, 1)

            def make_onehot(J, col, slot):
                dve.wait_ge(step_summed, (J - 1) * GROUP + CREDIT)
                nc.vector.tensor_tensor(onehot[:, slot, :, :], iota_free[:].unsqueeze(1).broadcast_to([P, GROUP, P]),
                                        loc[:, bass.ds(col, GROUP)].unsqueeze(2).broadcast_to([P, GROUP, P]),
                                        ALU.is_equal).then_inc(onehot_ready, 1)

            def add_steps(q, i, h, target, width):
                tiles = step_tiles(mybir.EngineType.DVE, i * RING + h)
                for s, n in enumerate(tiles):
                    g = ((q * BODIES + i) * RING + h) * GROUP + s
                    dve.wait_ge(step_summed, g + 1 + CREDIT)
                    dve.wait_ge(step_added, g + CREDIT)
                    nc.vector.tensor_tensor(target(n), target(n), agg[:, s, 0:width], ALU.add).then_inc(step_added, 1)

            dve.engine_nop().then_inc(step_added, CREDIT)
            nc.vector.tensor_tensor(onehot[:, 0, :, :], iota_free[:].unsqueeze(1).broadcast_to([P, GROUP, P]),
                                    loc[:, 0:GROUP].unsqueeze(2).broadcast_to([P, GROUP, P]), ALU.is_equal).then_inc(onehot_ready, 1)
            with dve.Fori(0, BODIES) as i:
                for h in range(RING):
                    make_onehot((Q_DEG * BODIES + i) * RING + h + 1, (i * RING + h + 1) * GROUP, (h + 1) % 2)
                    add_steps(Q_DEG, i, h, lambda n: degree[:, bass.ds(n, 1)], 1)
            dve.engine_nop().then_inc(deg_ready, 1)
            dve.wait_ge(cum_ready, 1)
            link(nc.vector.tensor_copy(cum[:, 0, :], dps[:, 1, 0:NT]))
            link(nc.vector.tensor_tensor_scan(cum[:, 1, :], ones[:, 0:NT], cum[:, 0, :], 0.0, ALU.mult, ALU.add))
            link(nc.vector.tensor_tensor(cum[:, 1, :], cum[:, 1, :], cum[:, 0, :], ALU.subtract))
            link(nc.vector.tensor_tensor(cum[:, 1, :], cum[:, 1, :], dps[:, 0, 0:NT], ALU.add))
            nc.vector.tensor_scalar(last_edge[:], cum[:, 1, :], -1.0, 0.0, ALU.add, ALU.max).then_inc(pos_ready, 1)
            link(nc.vector.tensor_tensor(cum[:, 0, :], cum[:, 1, :], degree[:, 0:NT], ALU.subtract))
            link(nc.vector.scalar_tensor_tensor(cum[:, 1, :], node_id[:], float(P * PER), cum[:, 0, :], ALU.add, ALU.subtract))
            link(nc.vector.tensor_scalar(rden[:, :, 0], degree[:, 0:NT], 0.0, None, ALU.is_equal))
            link(nc.vector.tensor_tensor(cum[:, 1, :], cum[:, 1, :], rden[:, :, 0], ALU.mult))
            link(nc.vector.tensor_tensor(first_edge[:], cum[:, 0, :], cum[:, 1, :], ALU.add))
            nc.vector.tensor_scalar(cum[:, 2, :], degree[:, 0:NT], 1.0, None, ALU.max).then_inc(plan_ready, 1)
            dve.wait_ge(std_ready, 2)
            link(nc.vector.reciprocal(dinv[:], dinv[:]))
            link(nc.vector.tensor_scalar(cum[:, 0, :], degree[:, 0:NT], 0.0, None, ALU.is_gt))
            link(nc.vector.tensor_tensor(dinv[:], dinv[:], cum[:, 0, :], ALU.mult))
            dve.wait_ge(s2_saved, SGROUPS)
            for hd in range(HEADS):
                last = nc.vector.tensor_tensor_scan(runmax[:, :, hd], fresh, s2e[:, :, hd], NEG, ALU.add, ALU.max)
            link(last)
            nc.vector.tensor_copy(carry[:, 0, 0:HEADS], runmax[:, PER - 1, :])
            link(nc.vector.tensor_reduce(carry_in[:, 0:1], fresh, AX.X, ALU.min))
            nc.vector.tensor_copy(carry[:, 1, 0:HEADS], carry_in[:, 0:1].broadcast_to([P, HEADS])).then_inc(carry_ready, 1)
            dve.wait_ge(carryT, 1)
            nc.vector.tensor_copy(carry_row[0:HEADS, 0, 0:P], tps[0:HEADS, 0, 0:P])
            nc.vector.memset(carry_row[0:HEADS, 2, 0:1], NEG)
            link(nc.vector.tensor_copy(carry_row[0:HEADS, 1, 0:P], tps[0:HEADS, 1, 0:P]))
            nc.vector.tensor_tensor_scan(carry_row[0:HEADS, 2, 1:P + 1], carry_row[0:HEADS, 1, 0:P], carry_row[0:HEADS, 0, 0:P],
                                         NEG, ALU.add, ALU.max).then_inc(carry_done, 1)
            dve.wait_ge(carry_back, 1)
            link(nc.vector.tensor_copy(carry_in[:, 0:HEADS], dps[:, 0, 0:HEADS]))
            for hd in range(HEADS):
                last = nc.vector.tensor_tensor_scan(runmax[:, :, hd], fresh, s2e[:, :, hd], carry_in[:, hd:hd + 1], ALU.add, ALU.max)
            last.then_inc(runmax_ready, 1)
            link(nc.vector.tensor_scalar(keep, fresh, 0.0, None, ALU.is_equal))
            link(nc.vector.tensor_tensor_scan(carried, keep, keep, 1.0, ALU.mult, ALU.min))
            dve.wait_ge(nbr_in, 16 * NT)
            link(nc.vector.tensor_tensor(nbr_max, nbr_max, node_sc[:, 0:NT, 0, :], ALU.add))
            nc.vector.scalar_tensor_tensor(node_sc[:, 0:NT, 1, :], nbr_max, 0.2, nbr_max, ALU.mult, ALU.max).then_inc(sc_ready, 1)
            dve.wait_ge(run_in, 16)
            for v in range(2 * HEADS):
                last = nc.vector.tensor_tensor_scan(run[:, :, v], keep, run[:, :, v], 0.0, ALU.mult, ALU.add)
            link(last)
            nc.vector.tensor_copy(carry[:, 0, :], run[:, PER - 1, :])
            nc.vector.tensor_copy(carry[:, 1, :], carried[:, PER - 1:PER].broadcast_to([P, 2 * HEADS])).then_inc(carry_ready, 1)
            dve.wait_ge(carryT, 2)
            nc.vector.tensor_copy(carry_row[:, 0, 0:P], tps[0:2 * HEADS, 0, 0:P])
            nc.vector.memset(carry_row[:, 2, 0:1], 0.0)
            link(nc.vector.tensor_copy(carry_row[:, 1, 0:P], tps[0:2 * HEADS, 1, 0:P]))
            nc.vector.tensor_tensor_scan(carry_row[:, 2, 1:P + 1], carry_row[:, 1, 0:P], carry_row[:, 0, 0:P],
                                         0.0, ALU.mult, ALU.add).then_inc(carry_done, 1)
            dve.wait_ge(carry_back, 2)
            link(nc.vector.tensor_copy(carry_in[:], dps[:, 0, 0:2 * HEADS]))
            for v in range(2 * HEADS):
                last = nc.vector.scalar_tensor_tensor(run[:, :, v], carried, carry_in[:, v:v + 1], run[:, :, v], ALU.mult, ALU.add)
            link(last)
            link(nc.vector.tensor_tensor(s2e, s2e, run[:, :, 0:HEADS], ALU.add))
            link(nc.vector.scalar_tensor_tensor(s2e, s2e, 0.2, s2e, ALU.mult, ALU.max))
            link(nc.vector.tensor_tensor(s2e, s2e, run[:, :, HEADS:2 * HEADS], ALU.subtract))
            nc.vector.tensor_scalar(s2e, s2e, 0.0, None, ALU.min).then_inc(gap_ready, 1)
            dve.wait_ge(pstep_ready, SC)
            dve.wait_ge(acc_clear, 1)
            def weight_rows(i, h):
                hh = rows[:, h * GROUP:(h + 1) * GROUP, 0:D].rearrange("p g (a o) -> p g a o", a=HEADS)
                dve.wait_ge(rows_landed[h], (i + 1) * (16 * GROUP))
                nc.vector.tensor_tensor(hh, hh, pstep[:, bass.ds((i * RING + h) * GROUP, GROUP), :].unsqueeze(3).broadcast_to([P, GROUP, HEADS, DH]),
                                        ALU.mult).then_inc(weighted, 1)

            def attention_body(i, more):
                for h in range(RING):
                    make_onehot((Q_ATT * BODIES + i) * RING + h + 1, (i * RING + h + 1) * GROUP, (h + 1) % 2)
                    if h + 1 < RING:
                        weight_rows(i, h + 1)
                    elif more:
                        weight_rows(i + 1, 0)
                    add_steps(Q_ATT, i, h, lambda n: ACC[:, bass.ds(n, 1), :], HD)

            weight_rows(0, 0)
            with dve.Fori(0, BODIES - 1) as i:
                attention_body(i, True)
            attention_body(BODIES - 1, False)
            link(nc.vector.tensor_scalar(rden, ACC[:, 0:NT, D:HD], 1e-30, None, ALU.max))
            link(nc.vector.reciprocal(rden, rden))
            a4v = ACC[:, 0:NT, 0:D].rearrange("p n (a o) -> p n a o", a=HEADS)
            link(nc.vector.tensor_tensor(a4v, a4v, rden.unsqueeze(3).broadcast_to([P, NT, HEADS, DH]), ALU.mult))
            nc.vector.scalar_tensor_tensor(res3, ACC[:, 0:NT, 0:D], 0.0, X[:], ALU.max, ALU.add).then_inc(acc_free, 1)
            dve.wait_ge(acc_free, 1)
            layernorm(res3)
            layernorm_end(3)
            with dve.Fori(0, NB) as i:
                dve.wait_ge(y_batch, i + 1)
                dve.nop(nofuse=True)
                for u in range(U):
                    n = i * U + u
                    dve.wait_ge(x0_ready, n + 1)
                    nc.vector.tensor_scalar(ybuf[:, u, 0:D], X[:, bass.ds(n, 1), :], dinv[:, bass.ds(n, 1)], None, ALU.mult).then_inc(y_ready, 1)
            dve.engine_nop().then_inc(g_x, 2)
            with dve.Fori(1, LAYERS + 1) as k:
                dve.wait_ge(acc_clear, (k - 1) * NT + 2)
                dve.nop(nofuse=True)
                with dve.Fori(0, BODIES) as i:
                    for h in range(RING):
                        make_onehot(((Q_LAYER - 1 + k) * BODIES + i) * RING + h + 1, (i * RING + h + 1) * GROUP, (h + 1) % 2)
                        add_steps(Q_LAYER - 1 + k, i, h, lambda n: ACC[:, bass.ds(n, 1), 0:D], D)
                dve.engine_nop().then_inc(passes_added, 1)
                dve.wait_ge(z_done, k * NT)
                dve.nop(nofuse=True)
                with dve.Fori(0, NB) as i:
                    dve.wait_ge(y_batch, k * NB + i + 1)
                    dve.nop(nofuse=True)
                    for u in range(U):
                        n = i * U + u
                        m = (k - 1) * NT + n
                        dve.wait_ge(g_ps, m + 3)
                        nc.vector.tensor_tensor(X[:, bass.ds(n, 1), :], X[:, bass.ds(n, 1), :], dps[:, u % 2, 0:D], ALU.add).then_inc(g_x, 1)
                        dve.wait_ge(g_x, m + 3)
                        nc.vector.tensor_scalar(ybuf[:, u, 0:D], X[:, bass.ds(n, 1), :], dinv[:, bass.ds(n, 1)], None, ALU.mult).then_inc(y_ready, 1)
            dve.wait_ge(y_ready, (LAYERS + 1) * NT)
            for c in range(U):
                t = slice(c * NB, (c + 1) * NB)
                nc.vector.tensor_tensor(X[:, t, :], X[:, t, :], res3[:, t, :], ALU.add).then_inc(out_ready, 1)

        @block.tensor
        def _(pe):
            for sem, credit in ((h_tr, 2), (proj_ready, 2), (g_tr, 2), (g_ps, 2), (step_summed, CREDIT)):
                pe.nop(nofuse=True).then_inc(sem, credit)
            pe.wait_ge(cmp_ready, 1)
            for ic in range(SC):
                for c in range(SC):
                    nc.tensor.matmul(dps[:, 0, ic:ic + 1], cmp[:, c, ic * P:(ic + 1) * P], ones_b[:], start=(c == 0), stop=(c == SC - 1))
            HS = SPAD // 2
            for b in range(2):
                for c in range(SC):
                    last = nc.tensor.matmul(tps[0:1, b, 0:HS], ones_b[:], cmp[:, c, b * HS:(b + 1) * HS], start=(c == 0), stop=(c == SC - 1))
            last.then_inc(counts_ready, 1)
            pe.wait_ge(steps_f, 1)
            for b in range(2):
                for c in range(4 * b, min(SC, 4 * b + 4)):
                    o = (c - 4 * b) * P
                    nc.tensor.transpose(agg[:, b, o:o + P], drowf[:, c, :], ident[:])
                    last = nc.tensor.transpose(agg[:, 2 + b, o:o + P], srowf[:, c, :], ident[:])
            last.then_inc(stepsT, 1)
            pe.wait_ge(wext_ready, 1)
            with pe.Fori(0, NB) as i:
                def turn(u):
                    n = i * U + u
                    pe.wait_ge(h_ready, n + 1)
                    pe.wait_ge(hT_ready, n + (2 if u == 0 else 1))
                    for c in range(2):
                        last = nc.tensor.transpose(tps[:, u % 2, c * P:(c + 1) * P], tileS[:, u % 2, c * P:(c + 1) * P], ident[:])
                    last.then_inc(h_tr, 1)

                turn(0)
                for u in range(U):
                    n = i * U + u
                    if u + 1 < U:
                        turn(u + 1)
                    pe.wait_ge(hT_ready, n + 3)
                    pe.wait_ge(proj_copied, n + (2 if u == 0 else 1))
                    for c in range(2):
                        last = nc.tensor.matmul(dps[:, u % 2, 0:PX], tileT[:, u % 2, c, :], wA[:, c, :], start=(c == 0), stop=(c == 1))
                    last.then_inc(proj_ready, 1)

            def sum_step(J, h, s, rhs, width):
                pe.wait_ge(step_added, J * GROUP + s + 1)
                nc.tensor.matmul(agg[:, s, 0:width], onehot[:, h % 2, s, :], rhs, start=True, stop=True).then_inc(step_summed, 1)

            with pe.Fori(0, BODIES) as i:
                for h in range(RING):
                    J = (Q_DEG * BODIES + i) * RING + h
                    pe.wait_ge(onehot_ready, J + 1)
                    for s in range(GROUP):
                        sum_step(J, h, s, ones[:, 0:1], 1)
            pe.wait_ge(deg_ready, 1)
            nc.tensor.matmul(dps[:, 0, 0:NT], tri, degree[:, 0:NT], start=True, stop=True)
            nc.tensor.matmul(dps[:, 1, 0:NT], ones[:], degree[:, 0:NT], start=True, stop=True).then_inc(cum_ready, 1)
            pe.wait_ge(carry_ready, 1)
            nc.tensor.transpose(tps[0:HEADS, 0, 0:P], carry[:, 0, 0:HEADS], ident[:])
            nc.tensor.transpose(tps[0:HEADS, 1, 0:P], carry[:, 1, 0:HEADS], ident[:]).then_inc(carryT, 1)
            pe.wait_ge(carry_done, 1)
            nc.tensor.transpose(dps[:, 0, 0:HEADS], carry_row[0:HEADS, 2, 0:P], ident[0:HEADS, 0:HEADS]).then_inc(carry_back, 1)

            pe.wait_ge(carry_ready, 2)
            nc.tensor.transpose(tps[0:2 * HEADS, 0, 0:P], carry[:, 0, :], ident[:])
            nc.tensor.transpose(tps[0:2 * HEADS, 1, 0:P], carry[:, 1, :], ident[:]).then_inc(carryT, 1)
            pe.wait_ge(carry_done, 2)
            nc.tensor.transpose(dps[:, 0, 0:2 * HEADS], carry_row[:, 2, 0:P], ident[0:2 * HEADS, 0:2 * HEADS]).then_inc(carry_back, 1)
            pe.wait_ge(prow_in, 16 * SC)
            for c in range(SC):
                if c >= GROUP:
                    pe.wait_ge(pstep_ready, c - GROUP + 1)
                for hd in range(HEADS):
                    last = nc.tensor.transpose(agg[:, c % GROUP, hd * P:(hd + 1) * P], prow[:, c, :, hd], ident[:])
                last.then_inc(prowT, 1)
            with pe.Fori(0, BODIES) as i:
                for h in range(RING):
                    j = i * RING + h
                    pe.wait_ge(onehot_ready, Q_ATT * GROUPS + j + 1)
                    pe.wait_ge(p_placed, j + 1)
                    pe.wait_ge(weighted, j + 1)
                    for s in range(GROUP):
                        sum_step(Q_ATT * GROUPS + j, h, s, rows[:, h * GROUP + s, :], HD)
            with pe.Fori(1, LAYERS + 1) as k:
                pe.wait_ge(w_layer, 32 * k)
                pe.nop(nofuse=True)

                def body(i, dense):
                    for h in range(RING):
                        J = ((Q_LAYER - 1 + k) * BODIES + i) * RING + h
                        m = (k - 1) * NT + i
                        pe.wait_ge(onehot_ready, J + 1)
                        pe.wait_ge(rows_landed[h], (k * BODIES + i + 1) * (16 * GROUP))
                        for s in range(GROUP):
                            sum_step(J, h, s, rows[:, h * GROUP + s, 0:D], D)
                        if dense and h == 1:
                            pe.wait_ge(z_copy, m + 1)
                            for c in range(2):
                                last = nc.tensor.transpose(tps[:, 0, c * P:(c + 1) * P], tileS[:, 0, c * P:(c + 1) * P], ident[:])
                            last.then_inc(z_tr, 1)
                        if dense and h == 2:
                            pe.wait_ge(z_copyT, m + 1)
                            for c in range(2):
                                last = nc.tensor.matmul(dps[:, 0, 0:D], tileT[:, 0, c, :], wA[:, c, 0:D], start=(c == 0), stop=(c == 1))
                            last.then_inc(z_ps, 1)

                with pe.Fori(0, NT) as i:
                    body(i, True)
                with pe.Fori(NT, BODIES) as i:
                    body(i, False)
                with pe.Fori(0, NB) as i:
                    def turn(u):
                        m = (k - 1) * NT + i * U + u
                        pe.wait_ge(g_copy, m + 1)
                        pe.wait_ge(g_copyT, m + (2 if u == 0 else 1))
                        for c in range(2):
                            last = nc.tensor.transpose(tps[:, u % 2, c * P:(c + 1) * P], tileS[:, u % 2, c * P:(c + 1) * P], ident[:])
                        last.then_inc(g_tr, 1)

                    turn(0)
                    for u in range(U):
                        m = (k - 1) * NT + i * U + u
                        if u + 1 < U:
                            turn(u + 1)
                        pe.wait_ge(g_copyT, m + 3)
                        pe.wait_ge(g_x, m + (2 if u == 0 else 1))
                        for c in range(2):
                            last = nc.tensor.matmul(dps[:, u % 2, 0:D], tileT[:, u % 2, c, :], wB[:, c, :], start=(c == 0), stop=(c == 1))
                        last.then_inc(g_ps, 1)


def kernel(x, src, dst, L0_gnn_W, L0_gnn_a, L1_gnn_W0, L1_gnn_W1):
    import numpy as np
    import concourse.bacc as bacc
    from concourse.bass_utils import run_bass_kernel_spmd

    nc = bacc.Bacc("TRN2", target_bir_lowering=False, num_devices=1)
    laid_out = {
        "x": np.asarray(x), "src": np.asarray(src), "dst": np.asarray(dst),
        "w_att": np.asarray(L0_gnn_W).transpose(1, 0, 2).reshape(D, HEADS * DH), "a_att": np.asarray(L0_gnn_a),
        "w0t": np.asarray(L1_gnn_W0).transpose(0, 2, 1), "w1t": np.asarray(L1_gnn_W1).transpose(0, 2, 1),
    }
    arrays, args = {}, []
    for name, a in laid_out.items():
        a = np.ascontiguousarray(a)
        arrays["in_" + name] = a
        args.append(nc.dram_tensor("in_" + name, a.shape, mybir.dt.from_np(a.dtype), kind="ExternalInput").ap())
    args.append(nc.dram_tensor("out_0", (N, D), F32, kind="ExternalOutput").ap())
    program(nc, *args)
    r = run_bass_kernel_spmd(nc, [arrays], core_ids=[0])
    return r.results[0]["out_0"]
```

```python
import concourse.bass as bass
from concourse import mybir

F32 = mybir.dt.float32
BF16 = mybir.dt.bfloat16
I32 = mybir.dt.int32
ALU = mybir.AluOpType
ACT = mybir.ActivationFunctionType
AX = mybir.AxisListType

P = 128
N, D = 6250, 256
HEADS, DH = 4, 64
E = 106250
LAYERS = 5
EPS = 1e-5
NT = -(-N // P)
LAST = N - (NT - 1) * P
ET = -(-E // P)
GROUP = 4
RING = 4
BODY = GROUP * RING
PER = 832
STEPS = PER
BODIES = STEPS // BODY
SC = -(-STEPS // P)
SPAD = SC * P
U = 7
NB = NT // U
PAIR = 2 * U
PAIRS = NT // PAIR
SENT = U * 16
HD = D + HEADS
PX = HD + HEADS
SU = 8
SGROUPS = PER // SU
FAR = 100000
NEG = -1e30
FULL, PART = (ET - 1) // P * P, (ET - 1) % P
REST = E - (ET - 1) * P
RUNS, RUNS_REST = E // PER, E % PER
BANKS = 4
CREDIT = BANKS
AHEAD = 2
W = 2 * P
DG = 4


def program(nc, x, src, dst, w_att, a_att, w0t, w1t, out):
    def sb(name, shape, dt=F32):
        return nc.alloc_sbuf_tensor(name, shape, dt)

    def dram(name, shape, dt=F32):
        return nc.dram_tensor(name, shape, dt, kind="Internal").ap()

    att_table = dram("att_table", (NT * P, D))
    score_table = dram("score_table", (NT * P, 2 * HEADS))
    p_table = dram("p_table", (STEPS, P * HEADS))
    y_table = dram("y_table", (NT * P, D))

    X = sb("X", [P, NT, D])
    RES = sb("RES", [P, NT * D])
    ACC = sb("ACC", [P, (NT + 1) * HD])
    rows = sb("rows", [P, BODY, HD])
    onehot = sb("onehot", [P, BANKS, W])
    loc = sb("loc", [P, SPAD])
    gidx = sb("gidx", [P, SPAD], I32)
    node_scores = sb("node_scores", [P, NT, 2 * HEADS])
    gidx_now = sb("gidx_now", [P, RING, GROUP], I32)
    ntile = sb("ntile", [1, SPAD], I32)
    wA = sb("wA", [P, 2, PX])
    wB = sb("wB", [P, 2, D])
    ybuf = sb("ybuf", [P, U, HD])
    tileS = sb("tileS", [P, 2, D])
    tileT = sb("tileT", [P, 2, 2, P])
    iota_free = sb("iota_free", [P, W])
    ident = sb("ident", [P, P])
    ones = sb("ones", [P, P])
    zeros_b = sb("zeros_b", [P, P], BF16)
    first_f = sb("first_f", [P, 2, SC])
    first_i = sb("first_i", [P, SC], I32)
    degree = sb("degree", [P, NT])
    dinv = sb("dinv", [P, NT])
    meanvar = sb("meanvar", [P, NT, 2])
    rstd = sb("rstd", [P, NT])
    shift = sb("shift", [P, NT])
    carry = sb("carry", [P, 4, 2 * HEADS])
    carry_row = sb("carry_row", [2 * HEADS, 6, P])
    carry_in = sb("carry_in", [P, 3, HEADS])

    accf = ACC[:]
    at = [0]

    def tmp(words):
        at[0] += words
        return accf[:, at[0] - words:at[0]]

    dchk = tmp(SPAD).bitcast(I32).rearrange("p (c e) -> p c e", c=SC)
    schk = tmp(SPAD).bitcast(I32).rearrange("p (c e) -> p c e", c=SC)
    srowf = tmp(SPAD).rearrange("p (c e) -> p c e", c=SC)
    drowf = tmp(SPAD).rearrange("p (c e) -> p c e", c=SC)
    locf = tmp(SPAD).rearrange("p (c e) -> p c e", c=SC)
    dst_i = tmp(STEPS).bitcast(I32)
    drowi = tmp(2 * STEPS).bitcast(I32).rearrange("p (k i) -> p k i", k=2)
    dnext = tmp(PER).bitcast(I32)
    a_bc = tmp(HEADS * 2 * DH)
    prod = tmp(D)
    scores = RES[:, 0:2 * PER * HEADS].rearrange("p (j h) -> p j h", h=2 * HEADS)
    fore, back, own = [accf[:, k * PER * HEADS:(k + 1) * PER * HEADS].rearrange("p (j h) -> p j h", h=HEADS) for k in range(3)]
    o = 2 * PER * HEADS
    starts = RES[:, o:o + PER]
    o += PER
    sidx = RES[:, o:o + PER + 2 * SU].bitcast(I32)
    o += PER + 2 * SU
    dcur = RES[:, o:o + PER].bitcast(I32)
    inner = RES[:, o:o + PER]
    dprev = RES[:, o + PER:o + 2 * PER].bitcast(I32)
    ends = RES[:, o + PER:o + 2 * PER]
    prow = RES[:, SPAD * HEADS:2 * SPAD * HEADS].rearrange("p (c e h) -> p c e h", c=SC, h=HEADS)
    pflat = RES[:, 0:SPAD * HEADS]
    pstep = pflat.rearrange("p (i h) -> p i h", h=HEADS)
    o += 2 * PER

    def rest(words):
        nonlocal o
        o += words
        return RES[:, o - words:o]

    known = rest(NT)
    rden = rest(NT * HEADS).rearrange("p (n h) -> p n h", h=HEADS)
    score_rows = rest(4 * SU * HEADS).rearrange("p (b u h) -> p b u h", b=2, u=SU)
    score_idx = rest(2 * SU).bitcast(I32).rearrange("p (b u) -> p b u", b=2)
    dst_lo, dst_hi = rest(STEPS), rest(STEPS)
    dw = DG * (P + NT)
    deg_hot = rows[:].rearrange("p b f -> p (b f)")[:, 0:2 * dw // 2].bitcast(BF16).rearrange("p (b w) -> p b w", b=2)
    hot_lo = deg_hot[:, :, 0:DG * P].rearrange("p b (s m) -> p b s m", m=P)
    hot_hi = deg_hot[:, :, DG * P:dw].rearrange("p b (s m) -> p b s m", m=NT)
    acc_nodes = ACC[:].rearrange("p (n f) -> p n f", f=HD)
    acc_feats = ACC[:, 0:(NT + 1) * D].rearrange("p (c n m) -> p c n m", c=2, m=P)
    stats = ybuf[:].rearrange("p u f -> p (u f)")[:, 0:NT * 6].rearrange("p (n k) -> p n k", k=6)
    res3 = RES[:].rearrange("p (n f) -> p n f", f=D)

    sums_now = [rows[:, u, 0:D].rearrange("p (c m) -> p c m", c=2) for u in range(U)]

    psum = nc.alloc_psum_tensor("psum", [P, 2 * BANKS, 512], F32)
    agg, tps, dps = psum[:, 0:BANKS, :], psum[:, BANKS:BANKS + 2, :], psum[:, BANKS + 2:BANKS + 4, :]

    stage_ps = [agg[:, b, 0:D] for b in range(4)] + [tps[:, 0, 0:D], tps[:, 1, 0:D], dps[:, 1, 0:D]]

    S = nc.alloc_semaphore
    cleared, consts = S("cleared"), S("consts")
    edge_in, x_in, w_in, a_in, lay_in = S("edge_in"), [S("x_in0"), S("x_in1")], S("w_in"), S("a_in"), S("lay_in")
    dve_step, pool_step = S("dve_step"), S("pool_step")
    steps_f, stepsT, steps_copied = S("steps_f"), S("stepsT"), S("steps_copied")
    hot_ready, hot_counted = S("hot_ready"), S("hot_counted")
    plan_ready = S("plan_ready")
    wext_ready = S("wext_ready")
    var_ready, std_ready, norm_ready = S("var_ready"), S("std_ready"), S("norm_ready")
    scores_done, score_sent = S("scores_done"), S("score_sent")
    a_ready, a_tr, aT_ready, a_ps = S("a_ready"), S("a_tr"), S("aT_ready"), S("a_ps")
    h_ready, h_tr, hT_ready, proj_ready, proj_copied, att_sent = (
        S("h_ready"), S("h_tr"), S("hT_ready"), S("proj_ready"), S("proj_copied"), [S("att_sent0"), S("att_sent1")])
    score_idx_ready, scores_saved = S("score_idx_ready"), S("scores_saved")
    scores_landed = [S("scores_landed0"), S("scores_landed1")]
    onehot_ready, step_summed, step_added = S("onehot_ready"), S("step_summed"), S("step_added")
    idx_ready = S("idx_ready")
    rows_landed = [S(f"rows_landed{h}") for h in range(RING)]
    deg_ready = S("deg_ready")
    carry_ready, carryT, carry_done, carry_back = S("carry_ready"), S("carryT"), S("carry_done"), S("carry_back")
    p_ready, p_out, prow_in, prowT, pstep_ready, p_placed, weighted, weighted_last = (
        S("p_ready"), S("p_out"), S("prow_in"), S("prowT"), S("pstep_ready"), S("p_placed"), S("weighted"), S("weighted_last"))
    gap_ready = S("gap_ready")
    acc_free, acc_clear = S("acc_free"), S("acc_clear")
    x0_ready, y_ready, y_sent = S("x0_ready"), S("y_ready"), [S("y_sent0"), S("y_sent1")]
    w_layer = S("w_layer")
    z_copy, z_tr, z_copyT, z_ps, z_done = S("z_copy"), S("z_tr"), S("z_copyT"), S("z_ps"), S("z_done")
    passes_added = S("passes_added")
    g_copy, g_ps, g_x = S("g_copy"), S("g_ps"), S("g_x")
    out_ready, out_sent = S("out_ready"), S("out_sent")

    Q_ATT, Q_LAYER = 0, 1

    def step_tiles(engine, body):
        _, tiles = nc.values_load_multi_w_load_instructions(
            ntile[0:1, bass.ds(body * BODY, BODY)], engines=(engine,), min_val=0, max_val=NT - 1,
            skip_runtime_bounds_check_because="a node's tile, held under NT when the windows are made")
        return tiles

    def y_slot(u):
        return ybuf[:, u, :] if u < U else rows[:, BODY // 2 + u - U, :]

    def all_tiles(engine, body, peel):
        if peel:
            body(0, PAIR)
        with engine.Fori(1 if peel else 0, PAIRS) as i:
            body(i, PAIR)
        body(PAIRS, U)

    with nc.Block() as block:

        @block.sync
        def _(sp):
            HALF = NB // 2 * U
            sp.dma_start(X[:, 0:HALF, :], x[0:HALF * P, :].rearrange("(n p) f -> p n f", p=P)).then_inc(x_in[0], 16)
            sp.dma_start(wA[:, :, 0:D], w_att.rearrange("(c p) f -> p c f", p=P)).then_inc(w_in, 16)
            sp.dma_start(a_bc, a_att.rearrange("h o -> (h o)").partition_broadcast(P)).then_inc(a_in, 16)
            sp.wait_ge(cleared, 1)
            for v, chk in ((dst, dchk), (src, schk)):
                sp.dma_start(chk[:, 0:SC - 1, :], v[0:FULL * P].rearrange("(c p e) -> p c e", p=P, e=P)).then_inc(edge_in, 16)
                sp.dma_start(chk[0:PART, SC - 1, :], v[FULL * P:(FULL + PART) * P].rearrange("(p e) -> p e", e=P)).then_inc(edge_in, 16)
                sp.dma_start(chk[PART:PART + 1, SC - 1, 0:REST], v[(ET - 1) * P:E].rearrange("(p e) -> p e", p=1)).then_inc(edge_in, 16)
            sp.dma_start(X[:, HALF:NT - 1, :], x[HALF * P:(NT - 1) * P, :].rearrange("(n p) f -> p n f", p=P)).then_inc(x_in[1], 16)
            sp.dma_start(X[0:LAST, NT - 1, :], x[(NT - 1) * P:N, :]).then_inc(x_in[1], 16)
            for v, lay in ((src, sidx), (dst, dcur)):
                sp.dma_start(lay[0:RUNS, 0:PER], v[0:RUNS * PER].rearrange("(p j) -> p j", j=PER)).then_inc(lay_in, 16)
                sp.dma_start(lay[RUNS:RUNS + 1, 0:RUNS_REST], v[RUNS * PER:E].rearrange("(p j) -> p j", p=1)).then_inc(lay_in, 16)
            sp.dma_start(dprev[0:1, 1:PER], dst[0:PER - 1].rearrange("(p j) -> p j", p=1)).then_inc(lay_in, 16)
            sp.dma_start(dprev[1:RUNS, :], dst[PER - 1:RUNS * PER - 1].rearrange("(p j) -> p j", j=PER)).then_inc(lay_in, 16)
            sp.dma_start(dprev[RUNS:RUNS + 1, 0:RUNS_REST + 1], dst[RUNS * PER - 1:E].rearrange("(p j) -> p j", p=1)).then_inc(lay_in, 16)
            sp.dma_start(dnext[0:RUNS, :], dst[1:RUNS * PER + 1].rearrange("(p j) -> p j", j=PER)).then_inc(lay_in, 16)
            sp.dma_start(dnext[RUNS:RUNS + 1, 0:RUNS_REST - 1], dst[RUNS * PER + 1:E].rearrange("(p j) -> p j", p=1)).then_inc(lay_in, 16)
            for t0, t1 in ((0, 4 * U), (4 * U, NT)):
                sp.wait_ge(scores_done, t1 + 2)
                sp.dma_start(score_table[t0 * P:t1 * P, :].rearrange("(n p) h -> p n h", p=P), node_scores[:, t0:t1, :]).then_inc(score_sent, 16)

            def send_att(i, count):
                for u in range(count):
                    n = i * PAIR + u
                    sp.wait_ge(proj_copied, n + 1 + 2)
                    sp.dma_start(att_table[bass.ds(n * P, P), :], y_slot(u)[:, 0:D]).then_inc(att_sent[u // U], 16)

            all_tiles(sp, send_att, False)
            sp.wait_ge(p_ready, 1)
            sp.dma_start(p_table.rearrange("r (e h) -> (r e) h", h=HEADS).rearrange("(p j) h -> p j h", p=P), back).then_inc(p_out, 16)
            sp.wait_ge(p_out, 16)
            for c in range(SC):
                w = min(P, STEPS - c * P)
                sp.dma_start(prow[0:w, c, :, :].rearrange("p e h -> p (e h)"), p_table[c * P:c * P + w, :]).then_inc(prow_in, 16)
            sp.dma_start(wB[:], w1t[0:1].rearrange("l (c p) f -> p (l c) f", p=P)).then_inc(w_layer, 16)
            sp.wait_ge(a_ps, NT + 2)
            sp.dma_start(wA[:, :, 0:D], w0t[0:1].rearrange("l (c p) f -> p (l c) f", p=P)).then_inc(w_layer, 16)

            def send_y(k):
                def send(i, count):
                    for u in range(count):
                        n = i * PAIR + u
                        sp.wait_ge(y_ready, k * NT + n + 1)
                        sp.dma_start(y_table[bass.ds(n * P, P), :], y_slot(u)[:, 0:D]).then_inc(y_sent[u // U], 16)

                all_tiles(sp, send, False)

            send_y(0)
            with sp.Fori(1, LAYERS) as k:
                send_y(k)
                sp.wait_ge(g_ps, k * NT + U)
                sp.dma_start(wA[:, :, 0:D], w0t[bass.ds(k, 1)].rearrange("l (c p) f -> p (l c) f", p=P)).then_inc(w_layer, 16)
                sp.dma_start(wB[:], w1t[bass.ds(k, 1)].rearrange("l (c p) f -> p (l c) f", p=P)).then_inc(w_layer, 16)
            for c in range(U):
                sp.wait_ge(out_ready, (c + 1) * U)
                t0, t1 = c * NB, (c + 1) * NB
                if c < U - 1:
                    sp.dma_start(out[t0 * P:t1 * P, :].rearrange("(n p) f -> p n f", p=P), X[:, t0:t1, :]).then_inc(out_sent, 16)
                else:
                    sp.dma_start(out[t0 * P:(NT - 1) * P, :].rearrange("(n p) f -> p n f", p=P), X[:, t0:NT - 1, :]).then_inc(out_sent, 16)
                    sp.dma_start(out[(NT - 1) * P:N, :], X[0:LAST, NT - 1, :]).then_inc(out_sent, 16)
            sp.wait_ge(out_sent, 16 * (U + 1))

        @block.gpsimd
        def _(pool):
            pool.iota(iota_free[:], [[1, W]], base=0, channel_multiplier=0, allow_small_or_imprecise_dtypes=True)
            pool.memset(ident[:], 0.0).then_inc(pool_step, 1)
            pool.wait_ge(pool_step, 1)
            pool.affine_select(out=ident[:], in_=ident[:], compare_op=ALU.not_equal, fill=1.0, base=0,
                               pattern=[[-1, P]], channel_multiplier=1).then_inc(consts, 1)
            pool.wait_ge(score_sent, 32)
            with pool.Fori(0, SGROUPS // 2) as i:
                for h in range(2):
                    pool.wait_ge(score_idx_ready, 2 * i + h + 1)
                    pool.nop(nofuse=True)
                    for u in range(SU):
                        pool.indirect_dma_start(score_rows[:, h, u, :], None, score_table,
                                                bass.IndirectOffsetOnAxis(ap=score_idx[:, h, u:u + 1], axis=0)).then_inc(scores_landed[h], 16)

            def gather(q, table, width):
                with pool.Fori(0, BODIES) as i:
                    for h in range(RING):
                        pool.wait_ge(idx_ready, (q * BODIES + i) * RING + h + 1)
                        pool.nop(nofuse=True)
                        for u in range(GROUP):
                            pool.indirect_dma_start(rows[:, h * GROUP + u, 0:width], None, table,
                                                    bass.IndirectOffsetOnAxis(ap=gidx_now[:, h, u:u + 1], axis=0)).then_inc(rows_landed[h], 16)

            pool.wait_ge(att_sent[0], SENT * (PAIRS + 1))
            pool.wait_ge(att_sent[1], SENT * PAIRS)
            gather(0, att_table, D)
            pool.wait_ge(acc_free, 1)
            pool.memset(ACC[:], 0.0).then_inc(acc_clear, 1)

            def gather_layer(k):
                pool.wait_ge(y_sent[0], k * (SENT * (PAIRS + 1)))
                pool.wait_ge(y_sent[1], k * (SENT * PAIRS))
                pool.nop(nofuse=True)
                gather(k, y_table, D)

            with pool.Fori(1, LAYERS) as k:
                gather_layer(k)
                for i in range(NB):
                    pool.wait_ge(g_copy, (k - 1) * NT + (i + 1) * U)
                    pool.nop(nofuse=True)
                    pool.memset(acc_feats[:, :, i * U:(i + 1) * U, :], 0.0).then_inc(acc_clear, 1)
            gather_layer(LAYERS)

        @block.scalar
        def _(act):
            act.wait_ge(var_ready, 1)
            act.activation(rstd[:], rstd[:], ACT.Sqrt).then_inc(std_ready, 1)
            act.wait_ge(norm_ready, 1)

            def normalised_tiles(i, count):
                def normalise(u):
                    n = i * PAIR + u
                    act.wait_ge(h_tr, n + 1)
                    act.nop(nofuse=True)
                    act.activation(tileS[:, u % 2, :], X[:, bass.ds(n, 1), :], ACT.Relu, bias=shift[:, bass.ds(n, 1)],
                                   scale=rstd[:, bass.ds(n, 1)]).then_inc(h_ready, 1)

                for u in range(count):
                    normalise(u)

            all_tiles(act, normalised_tiles, False)
            act.wait_ge(lay_in, 144)
            for h in range(2):
                act.activation(score_idx[:, h, :], sidx[:, h * SU:(h + 1) * SU], ACT.Copy).then_inc(score_idx_ready, 1)
            with act.Fori(0, SGROUPS // 2) as i:
                for h in range(2):
                    act.wait_ge(scores_landed[h], (i + 1) * (16 * SU))
                    act.nop(nofuse=True)
                    act.activation(scores[:, bass.ds((2 * i + h) * SU, SU), :], score_rows[:, h, :, :], ACT.Copy).then_inc(scores_saved, 1)
                    act.activation(score_idx[:, h, :], sidx[:, bass.ds((2 * i + h + 2) * SU, SU)], ACT.Copy).then_inc(score_idx_ready, 1)
            act.wait_ge(plan_ready, 1)
            act.activation(dinv[:], dinv[:], ACT.Sqrt).then_inc(std_ready, 1)
            for h in range(RING):
                act.activation(gidx_now[:, h, :], gidx[:, h * GROUP:(h + 1) * GROUP], ACT.Copy).then_inc(idx_ready, 1)

            def next_index(q, i, h):
                act.wait_ge(step_summed, ((q * BODIES + i) * RING + h + 1) * GROUP + CREDIT)
                act.nop(nofuse=True)
                act.activation(gidx_now[:, h, :], gidx[:, bass.ds((i * RING + h + RING) * GROUP, GROUP)], ACT.Copy).then_inc(idx_ready, 1)

            act.wait_ge(gap_ready, 1)
            act.activation(back, back, ACT.Exp).then_inc(p_ready, 1)
            for c in range(SC):
                act.wait_ge(prowT, c + 1)
                w = min(P, STEPS - c * P)
                act.activation(pstep[:, c * P:c * P + w, :], agg[:, c % BANKS, :].rearrange("p (h i) -> p i h", h=HEADS)[:, 0:w, :], ACT.Copy).then_inc(pstep_ready, 1)
            act.wait_ge(pstep_ready, SC)

            def weight_rows(i, h):
                j = i * RING + h
                act.activation(rows[:, h * GROUP:(h + 1) * GROUP, D:HD], pstep[:, bass.ds(j * GROUP, GROUP), :], ACT.Copy).then_inc(p_placed, 1)
                act.wait_ge(rows_landed[h], (i + 1) * (16 * GROUP))
                act.nop(nofuse=True)
                for s in range(GROUP):
                    for hd in range(HEADS - 1):
                        r = rows[:, h * GROUP + s, hd * DH:(hd + 1) * DH]
                        last = act.activation(r, r, ACT.Copy, scale=pflat[:, bass.ds((j * GROUP + s) * HEADS + hd, 1)])
                last.then_inc(weighted, 1)

            def attention_body(i, more):
                for h in range(RING):
                    if h + 1 < RING:
                        weight_rows(i, h + 1)
                    elif more:
                        weight_rows(i + 1, 0)
                    next_index(Q_ATT, i, h)

            weight_rows(0, 0)
            with act.Fori(0, BODIES - 1) as i:
                attention_body(i, True)
            attention_body(BODIES - 1, False)
            act.wait_ge(var_ready, 2)
            act.activation(rstd[:], rstd[:], ACT.Sqrt).then_inc(std_ready, 1)
            act.wait_ge(norm_ready, 2)
            with act.Fori(0, NB) as i:
                for u in range(U):
                    n = i * U + u
                    act.activation(X[:, bass.ds(n, 1), :], res3[:, bass.ds(n, 1), :], ACT.Relu, bias=shift[:, bass.ds(n, 1)],
                                   scale=rstd[:, bass.ds(n, 1)]).then_inc(x0_ready, 1)
            act.wait_ge(x0_ready, NT)
            with act.Fori(1, LAYERS + 1) as k:
                act.wait_ge(g_x, (k - 1) * NT + U)
                act.nop(nofuse=True)

                def body(i, dense):
                    for h in range(RING):
                        next_index(Q_LAYER - 1 + k, i, h)
                        m = k * NT - NT + i
                        if dense and h == 0:
                            act.activation(tileS[:, 0, :], X[:, bass.ds(i, 1), :], ACT.Copy).then_inc(z_copy, 1)
                        if dense and h == 1:
                            act.wait_ge(z_tr, m + 1)
                            act.activation(tileT[:, 0, :, :], tps[:, 0, 0:D].rearrange("p (c m) -> p c m", c=2), ACT.Copy).then_inc(z_copyT, 1)
                        if dense and h == 2:
                            act.wait_ge(z_ps, m + 1)
                            act.nop(nofuse=True)
                            act.activation(X[:, bass.ds(i, 1), :], dps[:, 0, 0:D], ACT.Copy).then_inc(z_done, 1)

                with act.Fori(0, NT) as i:
                    body(i, True)
                with act.Fori(NT, BODIES) as i:
                    body(i, False)
                act.wait_ge(passes_added, k)
                act.nop(nofuse=True)
                with act.Fori(0, NB) as i:
                    for u in range(U):
                        n = i * U + u
                        act.wait_ge(g_ps, (k - 1) * NT + n + 1)
                        act.nop(nofuse=True)
                        act.activation(sums_now[u], acc_feats[:, :, bass.ds(n, 1), :], ACT.Copy).then_inc(g_copy, 1)

        @block.vector
        def _(dve):
            links = [0]

            def link(ins):
                links[0] += 1
                ins.then_inc(dve_step, 1)
                dve.wait_ge(dve_step, links[0])

            nc.vector.memset(dchk[:, SC - 1, :], FAR)
            nc.vector.memset(sidx, 0)
            nc.vector.memset(dcur, FAR)
            nc.vector.memset(dprev, FAR)
            nc.vector.memset(dnext, FAR)
            nc.vector.memset(X[:, NT - 1, :], 0.0)
            nc.vector.memset(ones[:], 1.0)
            nc.vector.memset(zeros_b[:], 0.0)
            nc.vector.memset(schk[:, SC - 1, :], 0).then_inc(cleared, 1)
            for sem in (hT_ready, scores_done, aT_ready, proj_copied):
                dve.engine_nop().then_inc(sem, 2)

            def statistics(tiles, first, end):
                with dve.Fori(first, end) as i:
                    for u in range(U):
                        nc.vector.bn_stats(stats[:, bass.ds(i * U + u, 1), :], tiles[:, bass.ds(i * U + u, 1), :])

            def layernorm():
                link(dve.engine_nop())
                mean, var = meanvar[:, :, 0], meanvar[:, :, 1]
                link(nc.vector.tensor_tensor(var, stats[:, :, 1], stats[:, :, 4], ALU.subtract))
                link(nc.vector.tensor_tensor(var, var, var, ALU.mult))
                link(nc.vector.tensor_scalar(var, var, 0.25, EPS, ALU.mult, ALU.add))
                link(nc.vector.tensor_tensor(mean, stats[:, :, 2], stats[:, :, 5], ALU.add))
                link(nc.vector.scalar_tensor_tensor(rstd[:], mean, 1.0 / D, var, ALU.mult, ALU.add))
                link(nc.vector.tensor_tensor(mean, stats[:, :, 1], stats[:, :, 4], ALU.add))
                nc.vector.tensor_scalar(mean, mean, 0.5, None, ALU.mult).then_inc(var_ready, 1)

            def layernorm_end(count):
                dve.wait_ge(std_ready, count)
                link(nc.vector.reciprocal(rstd[:], rstd[:]))
                link(nc.vector.tensor_tensor(shift[:], meanvar[:, :, 0], rstd[:], ALU.mult))
                nc.vector.tensor_scalar(shift[:], shift[:], -1.0, None, ALU.mult).then_inc(norm_ready, 1)

            dve.wait_ge(edge_in, 96)
            dve.wait_ge(consts, 1)
            link(nc.vector.tensor_single_scalar(first_i[:], dchk[:, :, 0], 7, ALU.arith_shift_right))
            link(nc.vector.tensor_copy(first_f[:, 0, :], first_i[:]))
            link(nc.vector.tensor_scalar(first_f[:, 0, :], first_f[:, 0, :], float(NT - 1), None, ALU.min))
            nc.vector.tensor_scalar(first_f[:, 1, :], first_f[:, 0, :], -float(P), None, ALU.mult)
            nc.vector.tensor_copy(srowf, schk)
            link(nc.vector.tensor_copy(drowf, dchk))
            for c in range(SC):
                last = nc.vector.tensor_scalar(locf[:, c, :], drowf[:, c, :], first_f[:, 1, c:c + 1], None, ALU.add)
            last.then_inc(steps_f, 1)
            dve.wait_ge(w_in, 16)
            dve.wait_ge(a_in, 16)
            a4 = a_bc.rearrange("p (h s o) -> p h s o", h=HEADS, s=2)
            pr = prod.rearrange("p (h o) -> p h o", h=HEADS)
            for c in range(2):
                for half, col in ((1, D), (0, HD)):
                    link(nc.vector.tensor_tensor(pr, wA[:, c, 0:D].rearrange("p (h o) -> p h o", h=HEADS), a4[:, :, half, :], ALU.mult))
                    link(nc.vector.tensor_reduce(wA[:, c, col:col + HEADS], pr, AX.X, ALU.add))
            dve.engine_nop().then_inc(wext_ready, 1)
            dve.wait_ge(x_in[0], 16)
            statistics(X, 0, NB // 2)
            dve.wait_ge(x_in[1], 32)
            statistics(X, NB // 2, NB)
            layernorm()
            layernorm_end(1)
            dve.wait_ge(stepsT, 1)
            for b in range(2):
                w = (min(SC, 4 * b + 4) - 4 * b) * P
                nc.vector.tensor_copy(loc[:, b * 512:b * 512 + w], agg[:, b, 0:w])
                nc.vector.tensor_copy(gidx[:, b * 512:b * 512 + w], agg[:, 2 + b, 0:w])
                nc.vector.tensor_copy(ntile[:, b * 512:b * 512 + w], dps[0:1, b, 0:w])
                w = min(w, STEPS - b * 512)
                last = nc.vector.tensor_copy(dst_i[:, b * 512:b * 512 + w], tps[:, b, 0:w])
            last.then_inc(steps_copied, 1)
            dve.wait_ge(steps_copied, 1)
            def score_tiles(i, count):
                def save(u):
                    n = i * PAIR + u
                    dve.wait_ge(proj_ready, n + 3)
                    dve.nop(nofuse=True)
                    nc.vector.tensor_copy(node_scores[:, bass.ds(n, 1), :], dps[:, u % 2, 0:2 * HEADS]).then_inc(scores_done, 1)

                for u in range(count):
                    n = i * PAIR + u
                    dve.wait_ge(h_tr, n + 3)
                    dve.wait_ge(proj_ready, n + 1)
                    nc.vector.tensor_copy(tileT[:, u % 2, :, :], tps[:, u % 2, 0:D].rearrange("p (c m) -> p c m", c=2)).then_inc(hT_ready, 1)
                    if u > 0:
                        save(u - 1)
                save(count - 1)

            all_tiles(dve, score_tiles, False)

            nc.vector.tensor_copy(loc[:, STEPS:SPAD], loc[:, 0:SPAD - STEPS])
            nc.vector.tensor_copy(gidx[:, STEPS:SPAD], gidx[:, 0:SPAD - STEPS])
            nc.vector.tensor_single_scalar(drowi[:, 0, :], dst_i, P - 1, ALU.bitwise_and)
            link(nc.vector.tensor_single_scalar(drowi[:, 1, :], dst_i, 7, ALU.arith_shift_right))
            nc.vector.tensor_copy(dst_lo, drowi[:, 0, :])
            link(nc.vector.tensor_copy(dst_hi, drowi[:, 1, :]))
            dve.wait_ge(lay_in, 144)
            link(nc.vector.tensor_tensor(starts, dcur, dprev, ALU.not_equal))
            link(nc.vector.tensor_tensor(ends, dcur, dnext, ALU.not_equal))
            nc.vector.tensor_scalar(starts, starts, NEG, None, ALU.mult)
            nc.vector.tensor_scalar(inner, ends, 0.0, NEG, ALU.is_equal, ALU.mult)
            link(nc.vector.tensor_scalar(ends, ends, NEG, None, ALU.mult))
            def project(i, count):
                def normalise(u):
                    n = i * PAIR + u
                    dve.wait_ge(a_tr, n + 1)
                    nc.vector.tensor_scalar(tileS[:, u % 2, :], X[:, bass.ds(n, 1), :], rstd[:, bass.ds(n, 1)], shift[:, bass.ds(n, 1)],
                                            ALU.mult, ALU.add).then_inc(a_ready, 1)

                def save(u):
                    n = i * PAIR + u
                    if u % U == 0 and (not isinstance(i, int) or i > 0):
                        dve.wait_ge(att_sent[u // U], i * SENT)
                        dve.nop(nofuse=True)
                    dve.wait_ge(a_ps, n + 3)
                    nc.vector.tensor_copy(y_slot(u)[:, 0:D], dps[:, u % 2, 0:D]).then_inc(proj_copied, 1)

                normalise(0)
                for u in range(count):
                    n = i * PAIR + u
                    if u + 1 < count:
                        normalise(u + 1)
                    dve.wait_ge(a_tr, n + 3)
                    dve.wait_ge(a_ps, n + 1)
                    nc.vector.tensor_scalar(tileT[:, u % 2, :, :], tps[:, u % 2, 0:D].rearrange("p (c m) -> p c m", c=2), 0.0, None,
                                            ALU.max).then_inc(aT_ready, 1)
                    if u > 0:
                        save(u - 1)
                save(count - 1)

            all_tiles(dve, project, True)
            with dve.Fori(0, STEPS // DG // 2) as i:
                for b in range(2):
                    dve.wait_ge(hot_counted, 2 * i + b + 1)
                    col = bass.ds((2 * i + b) * DG, DG)
                    nc.vector.tensor_tensor(hot_lo[:, b, :, :], iota_free[:, 0:P].unsqueeze(1).broadcast_to([P, DG, P]),
                                            dst_lo[:, col].unsqueeze(2).broadcast_to([P, DG, P]), ALU.is_equal)
                    nc.vector.tensor_tensor(hot_hi[:, b, :, :], iota_free[:, 0:NT].unsqueeze(1).broadcast_to([P, DG, NT]),
                                            dst_hi[:, col].unsqueeze(2).broadcast_to([P, DG, NT]), ALU.is_equal).then_inc(hot_ready, 1)
            dve.wait_ge(hot_counted, STEPS // DG + 3)
            nc.vector.tensor_copy(degree[:], agg[:, 0, 0:NT]).then_inc(deg_ready, 1)
            dve.wait_ge(deg_ready, 1)

            def make_onehot(slot, col):
                nc.vector.tensor_scalar(onehot[:, slot, :], iota_free[:], loc[:, col], None, ALU.is_equal).then_inc(onehot_ready, 1)

            def step(q, i, s, n, add):
                T = (q * BODIES + i) * BODY + s
                dve.wait_ge(step_summed, T + AHEAD + 1)
                make_onehot((s + AHEAD) % BANKS, bass.ds(i * BODY + s + AHEAD, 1))
                dve.wait_ge(step_summed, T + 1 + CREDIT)
                dve.wait_ge(step_added, T + CREDIT)
                add(n, s % BANKS).then_inc(step_added, 1)

            def add_layer(n, b):
                t = acc_feats[:, :, bass.ds(n, 2), :]
                return nc.vector.tensor_tensor(t, t, agg[:, b, :].rearrange("p (c w m) -> p c w m", c=2, w=2), ALU.add)

            def add_attention(n, b):
                t = acc_nodes[:, bass.ds(n, 2), :]
                return nc.vector.tensor_tensor(t, t, psum[:, 2 * b:2 * b + 2, 0:HD], ALU.add)

            def sum_body(q, i, add, between=None):
                for s, n in enumerate(step_tiles(mybir.EngineType.DVE, i)):
                    step(q, i, s, n, add)
                    if between and s % GROUP == 0:
                        between(s // GROUP + 1)

            def weight_last(i, h):
                r = rows[:, h * GROUP:(h + 1) * GROUP, (HEADS - 1) * DH:D]
                dve.wait_ge(rows_landed[h], (i + 1) * (16 * GROUP))
                nc.vector.tensor_tensor(r, r, pstep[:, bass.ds((i * RING + h) * GROUP, GROUP), HEADS - 1:HEADS].broadcast_to([P, GROUP, DH]),
                                        ALU.mult).then_inc(weighted_last, 1)

            dve.engine_nop().then_inc(step_added, CREDIT)
            nc.vector.tensor_scalar(dinv[:], degree[:], 1.0, None, ALU.max).then_inc(plan_ready, 1)
            rev = slice(None, None, -1)
            s1 = scores[:, :, HEADS:2 * HEADS]
            EARLY = (SGROUPS - 8) * SU

            def fore_part(a, b):
                for hd in range(HEADS):
                    nc.vector.tensor_tensor_scan(fore[:, a:b, hd], starts[:, a:b], scores[:, a:b, hd],
                                                 NEG if a == 0 else fore[:, a - 1, hd:hd + 1], ALU.add, ALU.max)
                return nc.vector.tensor_tensor(s1[:, a:b, :], s1[:, a:b, :], inner[:, a:b].unsqueeze(2).broadcast_to([P, b - a, HEADS]), ALU.add)

            def scan_fore(hd, begin):
                return nc.vector.tensor_tensor_scan(fore[:, :, hd], starts, scores[:, :, hd], begin, ALU.add, ALU.max)

            def scan_back(hd, begin, begin_own):
                nc.vector.tensor_tensor_scan(back[:, rev, hd], ends[:, rev], scores[:, rev, hd], begin, ALU.add, ALU.max)
                return nc.vector.tensor_tensor_scan(own[:, rev, hd], ends[:, rev], scores[:, rev, HEADS + hd], begin_own, ALU.add, ALU.max)

            dve.wait_ge(scores_saved, EARLY // SU)
            nc.vector.tensor_reduce(carry_in[:, 0, 0:1], starts, AX.X, ALU.min)
            nc.vector.tensor_reduce(carry_in[:, 1, 0:1], ends, AX.X, ALU.min)
            link(fore_part(0, EARLY))
            dve.wait_ge(scores_saved, SGROUPS)
            link(fore_part(EARLY, PER))
            for hd in range(HEADS):
                last = scan_back(hd, NEG, NEG)
            link(last)
            nc.vector.tensor_copy(carry[:, 0, 0:HEADS], fore[:, PER - 1, :])
            nc.vector.tensor_copy(carry[:, 2, 0:HEADS], back[:, 0, :])
            nc.vector.tensor_copy(carry[:, 2, HEADS:2 * HEADS], own[:, 0, :])
            nc.vector.tensor_copy(carry[:, 1, 0:HEADS], carry_in[:, 0, 0:1].broadcast_to([P, HEADS]))
            nc.vector.tensor_copy(carry[:, 3, :], carry_in[:, 1, 0:1].broadcast_to([P, 2 * HEADS])).then_inc(carry_ready, 1)
            dve.wait_ge(carryT, 1)
            for v, ps in enumerate((tps[0:HEADS, 0, 0:P], tps[0:HEADS, 1, 0:P], None, dps[0:2 * HEADS, 0, 0:P], dps[0:2 * HEADS, 1, 0:P])):
                if ps is not None:
                    nc.vector.tensor_copy(carry_row[0:HEADS if v < 3 else 2 * HEADS, v, :], ps)
            nc.vector.memset(carry_row[0:HEADS, 2, 0:1], NEG)
            link(nc.vector.memset(carry_row[:, 5, P - 1:P], NEG))
            nc.vector.tensor_tensor_scan(carry_row[0:HEADS, 2, 1:P], carry_row[0:HEADS, 1, 0:P - 1], carry_row[0:HEADS, 0, 0:P - 1],
                                         NEG, ALU.add, ALU.max)
            nc.vector.tensor_tensor_scan(carry_row[:, 5, P - 2::-1], carry_row[:, 4, P - 1:0:-1], carry_row[:, 3, P - 1:0:-1],
                                         NEG, ALU.add, ALU.max).then_inc(carry_done, 1)
            dve.wait_ge(carry_back, 1)
            nc.vector.tensor_copy(carry_in[:, 0, :], tps[:, 0, 0:HEADS])
            link(nc.vector.tensor_copy(carry_in[:, 1:3, :], dps[:, 0, 0:2 * HEADS].rearrange("p (v h) -> p v h", h=HEADS)))
            for hd in range(HEADS):
                scan_fore(hd, carry_in[:, 0, hd:hd + 1])
                last = scan_back(hd, carry_in[:, 1, hd:hd + 1], carry_in[:, 2, hd:hd + 1])
            link(last)
            link(nc.vector.tensor_tensor(fore, fore, back, ALU.max))
            nc.vector.tensor_tensor(fore, fore, own, ALU.add)
            link(nc.vector.tensor_tensor(back, scores[:, :, 0:HEADS], own, ALU.add))
            nc.vector.scalar_tensor_tensor(fore, fore, 0.2, fore, ALU.mult, ALU.max)
            link(nc.vector.scalar_tensor_tensor(back, back, 0.2, back, ALU.mult, ALU.max))
            link(nc.vector.tensor_tensor(back, back, fore, ALU.subtract))
            nc.vector.tensor_scalar(back, back, 0.0, None, ALU.min).then_inc(gap_ready, 1)
            part = PER * HEADS
            dve.wait_ge(gap_ready, 1)
            nc.vector.memset(accf[:, 0:part], 0.0)
            nc.vector.memset(accf[:, 2 * part:(NT + 1) * HD], 0.0)
            dve.wait_ge(std_ready, 2)
            link(nc.vector.reciprocal(dinv[:], dinv[:]))
            link(nc.vector.tensor_scalar(known, degree[:], 0.0, None, ALU.is_gt))
            link(nc.vector.tensor_tensor(dinv[:], dinv[:], known, ALU.mult))
            dve.wait_ge(p_out, 16)
            nc.vector.memset(accf[:, part:2 * part], 0.0).then_inc(acc_clear, 1)
            dve.wait_ge(acc_clear, 1)
            for t in range(AHEAD):
                make_onehot(t, slice(t, t + 1))
            dve.wait_ge(pstep_ready, SC)
            weight_last(0, 0)
            with dve.Fori(0, BODIES - 1) as i:
                sum_body(Q_ATT, i, add_attention, lambda h: weight_last(i, h) if h < RING else weight_last(i + 1, 0))
            sum_body(Q_ATT, BODIES - 1, add_attention, lambda h: weight_last(BODIES - 1, h) if h < RING else None)
            dve.wait_ge(step_added, STEPS + CREDIT)
            link(nc.vector.tensor_scalar(rden, acc_nodes[:, 0:NT, D:HD], 1e-30, None, ALU.max))
            link(nc.vector.reciprocal(rden, rden))
            a4v = acc_nodes[:, 0:NT, 0:D].rearrange("p n (a o) -> p n a o", a=HEADS)
            link(nc.vector.tensor_tensor(a4v, a4v, rden.unsqueeze(3).broadcast_to([P, NT, HEADS, DH]), ALU.mult))
            nc.vector.scalar_tensor_tensor(res3, acc_nodes[:, 0:NT, 0:D], 0.0, X[:], ALU.max, ALU.add).then_inc(acc_free, 1)
            dve.wait_ge(acc_free, 1)
            statistics(res3, 0, NB)
            layernorm()
            layernorm_end(3)
            def first_table(i, count):
                for u in range(count):
                    n = i * PAIR + u
                    if u % U == 0 and (not isinstance(i, int) or i > 0):
                        dve.wait_ge(y_sent[u // U], i * SENT)
                        dve.nop(nofuse=True)
                    dve.wait_ge(x0_ready, n + 1)
                    nc.vector.tensor_scalar(y_slot(u)[:, 0:D], X[:, bass.ds(n, 1), :], dinv[:, bass.ds(n, 1)], None, ALU.mult).then_inc(y_ready, 1)

            all_tiles(dve, first_table, True)
            dve.engine_nop().then_inc(g_x, U)

            def layer(k, final):
                dve.wait_ge(acc_clear, (k - 1) * NB + 2)
                dve.nop(nofuse=True)
                with dve.Fori(0, BODIES) as i:
                    sum_body(Q_LAYER - 1 + k, i, add_layer)
                dve.wait_ge(step_added, (k + 1) * STEPS + CREDIT)
                dve.nop(nofuse=True).then_inc(passes_added, 1)
                dve.wait_ge(z_done, k * NT)
                dve.nop(nofuse=True)

                def update(i, count):
                    def follow(u):
                        n = i * PAIR + u
                        x_tile = X[:, bass.ds(n, 1), :]
                        if u % U == 0 and not final:
                            dve.wait_ge(y_sent[u // U], (k * (PAIRS + 1 - u // U) + i) * SENT)
                            dve.nop(nofuse=True)
                        dve.wait_ge(g_x, (k - 1) * NT + n + 1 + U)
                        if final:
                            nc.vector.tensor_tensor(x_tile, x_tile, res3[:, bass.ds(n, 1), :], ALU.add).then_inc(out_ready, 1)
                        else:
                            nc.vector.tensor_scalar(y_slot(u)[:, 0:D], x_tile, dinv[:, bass.ds(n, 1)], None, ALU.mult).then_inc(y_ready, 1)

                    for u in range(count):
                        n = i * PAIR + u
                        dve.wait_ge(g_ps, (k - 1) * NT + n + 1 + U)
                        nc.vector.scalar_tensor_tensor(X[:, bass.ds(n, 1), :], stage_ps[u % U], dinv[:, bass.ds(n, 1)], X[:, bass.ds(n, 1), :],
                                                       ALU.mult, ALU.add).then_inc(g_x, 1)
                        if u > 0:
                            follow(u - 1)
                    follow(count - 1)

                all_tiles(dve, update, False)

            with dve.Fori(1, LAYERS) as k:
                layer(k, False)
            layer(LAYERS, True)

        @block.tensor
        def _(pe):
            for sem, credit in ((h_tr, 2), (proj_ready, 2), (a_tr, 2), (a_ps, 2), (g_ps, U), (step_summed, CREDIT), (hot_counted, 2)):
                pe.nop(nofuse=True).then_inc(sem, credit)
            pe.wait_ge(steps_f, 1)
            for b in range(2):
                for c in range(4 * b, min(SC, 4 * b + 4)):
                    o = (c - 4 * b) * P
                    nc.tensor.transpose(agg[:, b, o:o + P], locf[:, c, :], ident[:])
                    nc.tensor.transpose(agg[:, 2 + b, o:o + P], srowf[:, c, :], ident[:])
                    nc.tensor.transpose(tps[:, b, o:o + P], drowf[:, c, :], ident[:])
                    last = nc.tensor.matmul(dps[0:1, b, o:o + P], first_f[:, 0, c:c + 1], ident[:], start=True, stop=True)
            last.then_inc(stepsT, 1)
            pe.wait_ge(wext_ready, 1)
            pe.wait_ge(steps_copied, 1)
            def project(ready, turned, copied, done, saved, columns):
                def tiles(i, count):
                    def turn(u):
                        n = i * PAIR + u
                        pe.wait_ge(ready, n + 1)
                        pe.wait_ge(copied, n + 1)
                        for c in range(2):
                            last = nc.tensor.transpose(tps[:, u % 2, c * P:(c + 1) * P], tileS[:, u % 2, c * P:(c + 1) * P], ident[:])
                        last.then_inc(turned, 1)

                    turn(0)
                    for u in range(count):
                        n = i * PAIR + u
                        if u + 1 < count:
                            turn(u + 1)
                        pe.wait_ge(copied, n + 3)
                        pe.wait_ge(saved, n + 1)
                        for c in range(2):
                            last = nc.tensor.matmul(dps[:, u % 2, 0:columns.stop - columns.start], tileT[:, u % 2, c, :], wA[:, c, columns],
                                                    start=(c == 0), stop=(c == 1))
                        last.then_inc(done, 1)

                all_tiles(pe, tiles, False)

            project(h_ready, h_tr, hT_ready, proj_ready, scores_done, slice(D, PX))
            project(a_ready, a_tr, aT_ready, a_ps, proj_copied, slice(0, D))
            pe.wait_ge(steps_copied, 1)
            nc.tensor.matmul(agg[:, 0, 0:NT], zeros_b[:], zeros_b[:, 0:NT], start=True, stop=False)
            with pe.Fori(0, STEPS // DG // 2) as i:
                for b in range(2):
                    pe.wait_ge(hot_ready, 2 * i + b + 1)
                    for s in range(DG):
                        last = nc.tensor.matmul(agg[:, 0, 0:NT], hot_lo[:, b, s, :], hot_hi[:, b, s, :], start=False, stop=False)
                    last.then_inc(hot_counted, 1)
            nc.tensor.matmul(agg[:, 0, 0:NT], zeros_b[:], zeros_b[:, 0:NT], start=False, stop=True).then_inc(hot_counted, 1)
            pe.wait_ge(deg_ready, 1)
            pe.wait_ge(carry_ready, 1)
            nc.tensor.transpose(tps[0:HEADS, 0, 0:P], carry[:, 0, 0:HEADS], ident[:])
            nc.tensor.transpose(tps[0:HEADS, 1, 0:P], carry[:, 1, 0:HEADS], ident[:])
            nc.tensor.transpose(dps[0:2 * HEADS, 0, 0:P], carry[:, 2, :], ident[:])
            nc.tensor.transpose(dps[0:2 * HEADS, 1, 0:P], carry[:, 3, :], ident[:]).then_inc(carryT, 1)
            pe.wait_ge(carry_done, 1)
            nc.tensor.transpose(tps[:, 0, 0:HEADS], carry_row[0:HEADS, 2, :], ident[0:HEADS, 0:HEADS])
            nc.tensor.transpose(dps[:, 0, 0:2 * HEADS], carry_row[:, 5, :], ident[0:2 * HEADS, 0:2 * HEADS]).then_inc(carry_back, 1)
            pe.wait_ge(prow_in, 16 * SC)
            for c in range(SC):
                if c >= BANKS:
                    pe.wait_ge(pstep_ready, c - BANKS + 1)
                w = min(P, STEPS - c * P)
                for hd in range(HEADS):
                    last = nc.tensor.transpose(agg[:, c % BANKS, hd * P:hd * P + w], prow[0:w, c, :, hd], ident[0:w, 0:w])
                last.then_inc(prowT, 1)
            pe.wait_ge(pstep_ready, SC)
            with pe.Fori(0, BODIES) as i:
                for h in range(RING):
                    pe.wait_ge(p_placed, i * RING + h + 1)
                    pe.wait_ge(weighted, i * RING + h + 1)
                    pe.wait_ge(weighted_last, i * RING + h + 1)
                    for s in range(GROUP):
                        T = (Q_ATT * BODIES + i) * BODY + h * GROUP + s
                        pe.wait_ge(onehot_ready, T + 1)
                        pe.wait_ge(step_added, T + 1)
                        for w in range(2):
                            last = nc.tensor.matmul(psum[:, 2 * s + w, 0:HD], onehot[:, s, w * P:(w + 1) * P], rows[:, h * GROUP + s, :],
                                                    start=True, stop=True)
                        last.then_inc(step_summed, 1)
            with pe.Fori(1, LAYERS + 1) as k:
                pe.wait_ge(w_layer, 32 * k)
                pe.nop(nofuse=True)

                def body(i, dense):
                    for h in range(RING):
                        m = (k - 1) * NT + i
                        pe.wait_ge(rows_landed[h], (k * BODIES + i + 1) * (16 * GROUP))
                        for s in range(GROUP):
                            T = ((Q_LAYER - 1 + k) * BODIES + i) * BODY + h * GROUP + s
                            pe.wait_ge(onehot_ready, T + 1)
                            pe.wait_ge(step_added, T + 1)
                            for c in range(2):
                                last = nc.tensor.matmul(agg[:, s, c * W:(c + 1) * W], rows[:, h * GROUP + s, c * P:(c + 1) * P], onehot[:, s, :],
                                                        start=True, stop=True)
                            last.then_inc(step_summed, 1)
                        if dense and h == 1:
                            pe.wait_ge(z_copy, m + 1)
                            for c in range(2):
                                last = nc.tensor.transpose(tps[:, 0, c * P:(c + 1) * P], tileS[:, 0, c * P:(c + 1) * P], ident[:])
                            last.then_inc(z_tr, 1)
                        if dense and h == 2:
                            pe.wait_ge(z_copyT, m + 1)
                            for c in range(2):
                                last = nc.tensor.matmul(dps[:, 0, 0:D], tileT[:, 0, c, :], wA[:, c, 0:D], start=(c == 0), stop=(c == 1))
                            last.then_inc(z_ps, 1)

                with pe.Fori(0, NT) as i:
                    body(i, True)
                with pe.Fori(NT, BODIES) as i:
                    body(i, False)
                with pe.Fori(0, NB) as i:
                    for u in range(U):
                        m = (k - 1) * NT + i * U + u
                        pe.wait_ge(g_copy, m + 1)
                        pe.wait_ge(g_x, m + 1)
                        for c in range(2):
                            last = nc.tensor.matmul(stage_ps[u], sums_now[u][:, c, :], wB[:, c, :], start=(c == 0), stop=(c == 1))
                        last.then_inc(g_ps, 1)


def kernel(x, src, dst, L0_gnn_W, L0_gnn_a, L1_gnn_W0, L1_gnn_W1):
    import numpy as np
    import concourse.bacc as bacc
    from concourse.bass_utils import run_bass_kernel_spmd

    nc = bacc.Bacc("TRN2", target_bir_lowering=False, num_devices=1)
    laid_out = {
        "x": np.asarray(x), "src": np.asarray(src), "dst": np.asarray(dst),
        "w_att": np.asarray(L0_gnn_W).transpose(1, 0, 2).reshape(D, HEADS * DH), "a_att": np.asarray(L0_gnn_a),
        "w0t": np.asarray(L1_gnn_W0).transpose(0, 2, 1), "w1t": np.asarray(L1_gnn_W1).transpose(0, 2, 1),
    }
    arrays, args = {}, []
    for name, a in laid_out.items():
        a = np.ascontiguousarray(a)
        arrays["in_" + name] = a
        args.append(nc.dram_tensor("in_" + name, a.shape, mybir.dt.from_np(a.dtype), kind="ExternalInput").ap())
    args.append(nc.dram_tensor("out_0", (N, D), F32, kind="ExternalOutput").ap())
    program(nc, *args)
    r = run_bass_kernel_spmd(nc, [arrays], core_ids=[0])
    return r.results[0]["out_0"]
```
